# Optimizing a Trainium2 kernel written in Bass

```python
import numpy as np
import jax
import jax.numpy as jnp

def _softmax(x, axis=-1):
    return jax.nn.softmax(x, axis=axis)

def _gelu(x):
    return jax.nn.gelu(x, approximate=True)

def _silu(x):
    return jax.nn.silu(x)

def _sigmoid(x):
    return jax.nn.sigmoid(x)

def _layernorm(x, axis=-1, eps=1e-05):
    m = jnp.mean(x, axis=axis, keepdims=True)
    v = jnp.var(x, axis=axis, keepdims=True)
    return (x - m) / jnp.sqrt(v + eps)

def _scatter_add(tgt, idx, src, axis=0):
    return tgt.at[idx].add(src)

def _segment_sum(src, seg, n):
    return jax.ops.segment_sum(src, seg, n)
kernel_name = 'mk_prb_d2_jaxref_r4_535290'

def setup_inputs(seed: int=0):
    np.random.seed(seed)
    _w = jnp.asarray

    def _L0_attn_setup():
        import jax, jax.numpy as jnp
        import numpy as np
        D_MODEL = 512
        SSM_RANK = 8
        FFN_RANK = D_MODEL // 64
        EPS = 1e-05

        def _layernorm(x, gamma, beta):
            mu = jnp.mean(x, axis=-1, keepdims=True)
            var = jnp.var(x, axis=-1, keepdims=True)
            return (x - mu) * jax.lax.rsqrt(var + EPS) * gamma + beta

        def _ssm_scan(u, decay):
            a = jnp.broadcast_to(decay, u.shape)

            def combine(e1, e2):
                a1, b1 = e1
                a2, b2 = e2
                return (a1 * a2, a2 * b1 + b2)
            _, h = jax.lax.associative_scan(combine, (a, u), axis=1)
            return h
        key = jax.random.key(seed)
        ks = jax.random.split(key, 10)
        d, r, rf = (D_MODEL, SSM_RANK, FFN_RANK)
        sc = 0.01
        return {'x': jax.random.normal(ks[0], (4, 1024, d), dtype=jnp.float32), 'ln_gamma': jnp.ones((d,), jnp.float32), 'ln_beta': jnp.zeros((d,), jnp.float32), 'W_in': jax.random.normal(ks[1], (d, r), jnp.float32) * (1.0 / np.sqrt(d)), 'b_in': jnp.zeros((r,), jnp.float32), 'decay_logit': jax.random.normal(ks[2], (r,), jnp.float32), 'W_out': jax.random.normal(ks[3], (r, d), jnp.float32) * (1.0 / np.sqrt(r)), 'b_out': jnp.zeros((d,), jnp.float32), 'D_skip': jax.random.normal(ks[4], (d,), jnp.float32) * 0.1, 'W_down': jax.random.normal(ks[5], (d, rf), jnp.float32) * sc, 'b_down': jnp.zeros((rf,), jnp.float32), 'W_up': jax.random.normal(ks[6], (rf, d), jnp.float32) * sc, 'b_up': jnp.zeros((d,), jnp.float32)}
    _L0_attn_in = _L0_attn_setup()

    def _L0_ffn_setup():
        import jax, jax.numpy as jnp
        import numpy as np
        B, S, D, H = (4, 512, 512, 2048)

        def fwht(x):
            orig_shape = x.shape
            n = orig_shape[-1]
            x = x.reshape(-1, n)
            h = 1
            while h < n:
                xb = x.reshape(-1, n // (2 * h), 2, h)
                a = xb[:, :, 0, :]
                b = xb[:, :, 1, :]
                x = jnp.stack([a + b, a - b], axis=2).reshape(-1, n)
                h *= 2
            scale = jnp.asarray(1.0 / np.sqrt(n), dtype=x.dtype)
            return (x * scale).reshape(orig_shape)
        key = jax.random.key(seed)
        kx, k1, k2, k3 = jax.random.split(key, 4)
        x = jax.random.normal(kx, (B, S, D), dtype=jnp.float32)
        W1 = jax.random.normal(k1, (H, D), dtype=jnp.float32) * (1.0 / np.sqrt(D))
        W2 = jax.random.normal(k2, (D, H), dtype=jnp.float32) * (1.0 / np.sqrt(H))
        W3 = jax.random.normal(k3, (H, D), dtype=jnp.float32) * (1.0 / np.sqrt(D))
        return {'x': x, 'W1': W1, 'W2': W2, 'W3': W3}
    _L0_ffn_in = _L0_ffn_setup()

    def _L1_attn_setup():
        import jax, jax.numpy as jnp
        import numpy as np
        D_MODEL = 512
        N_HEADS = 16
        HEAD_DIM = D_MODEL // N_HEADS
        key = jax.random.key(seed)
        ks = jax.random.split(key, 5)
        b, l, d = (2, 512, D_MODEL)
        x = jax.random.normal(ks[0], (b, l, d), dtype=jnp.float32)
        s_qkv = 1.0 / np.sqrt(d)
        W_qkv = jax.random.uniform(ks[1], (3 * d, d), dtype=jnp.float32, minval=-s_qkv, maxval=s_qkv)
        b_qkv = jax.random.uniform(ks[2], (3 * d,), dtype=jnp.float32, minval=-s_qkv, maxval=s_qkv)
        W_out = jax.random.uniform(ks[3], (d, d), dtype=jnp.float32, minval=-s_qkv, maxval=s_qkv)
        b_out = jax.random.uniform(ks[4], (d,), dtype=jnp.float32, minval=-s_qkv, maxval=s_qkv)
        return {'x': x, 'W_qkv': W_qkv, 'b_qkv': b_qkv, 'W_out': W_out, 'b_out': b_out}
    _L1_attn_in = _L1_attn_setup()

    def _L1_ffn_setup():
        import jax, jax.numpy as jnp
        import numpy as np

        def _sparsify_2to4(h):
            B, S, I = h.shape
            g = h.reshape(B, S, I // 4, 4)
            a = jnp.abs(g)
            _, idx = jax.lax.top_k(a, 2)
            pos = jnp.arange(4)
            mask = (pos == idx[..., 0:1]) | (pos == idx[..., 1:2])
            return (g * mask.astype(g.dtype)).reshape(B, S, I)
        key = jax.random.key(seed)
        k1, k2, k3, k4 = jax.random.split(key, 4)
        B, S, H, I = (4, 512, 512, 2048)
        x = jax.random.normal(k1, (B, S, H), dtype=jnp.float32)
        w_gate = jax.random.normal(k2, (H, I), dtype=jnp.float32) / np.sqrt(H)
        w_up = jax.random.normal(k3, (H, I), dtype=jnp.float32) / np.sqrt(H)
        w_down = jax.random.normal(k4, (I, H), dtype=jnp.float32) / np.sqrt(I)
        return {'x': x, 'w_gate': w_gate, 'w_up': w_up, 'w_down': w_down}
    _L1_ffn_in = _L1_ffn_setup()
    _d = {'L0_attn_x': _L0_attn_in['x'], 'L0_attn_ln_gamma': _L0_attn_in['ln_gamma'], 'L0_attn_ln_beta': _L0_attn_in['ln_beta'], 'L0_attn_W_in': _L0_attn_in['W_in'], 'L0_attn_b_in': _L0_attn_in['b_in'], 'L0_attn_decay_logit': _L0_attn_in['decay_logit'], 'L0_attn_W_out': _L0_attn_in['W_out'], 'L0_attn_b_out': _L0_attn_in['b_out'], 'L0_attn_D_skip': _L0_attn_in['D_skip'], 'L0_attn_W_down': _L0_attn_in['W_down'], 'L0_attn_b_down': _L0_attn_in['b_down'], 'L0_attn_W_up': _L0_attn_in['W_up'], 'L0_attn_b_up': _L0_attn_in['b_up'], 'L0_ffn_W1': _L0_ffn_in['W1'], 'L0_ffn_W2': _L0_ffn_in['W2'], 'L0_ffn_W3': _L0_ffn_in['W3'], 'L1_attn_W_qkv': _L1_attn_in['W_qkv'], 'L1_attn_b_qkv': _L1_attn_in['b_qkv'], 'L1_attn_W_out': _L1_attn_in['W_out'], 'L1_attn_b_out': _L1_attn_in['b_out'], 'L1_ffn_w_gate': _L1_ffn_in['w_gate'], 'L1_ffn_w_up': _L1_ffn_in['w_up'], 'L1_ffn_w_down': _L1_ffn_in['w_down']}
    _x0 = _d['L0_attn_x']
    _d['L0_attn_x'] = jax.random.normal(jax.random.fold_in(jax.random.key(seed), 1), (2, 1024, 512), dtype=_x0.dtype)
    del _x0
    return _d

def reference(L0_attn_x, L0_attn_ln_gamma, L0_attn_ln_beta, L0_attn_W_in, L0_attn_b_in, L0_attn_decay_logit, L0_attn_W_out, L0_attn_b_out, L0_attn_D_skip, L0_attn_W_down, L0_attn_b_down, L0_attn_W_up, L0_attn_b_up, L0_ffn_W1, L0_ffn_W2, L0_ffn_W3, L1_attn_W_qkv, L1_attn_b_qkv, L1_attn_W_out, L1_attn_b_out, L1_ffn_w_gate, L1_ffn_w_up, L1_ffn_w_down):

    def _L0_attn_ref(x, ln_gamma, ln_beta, W_in, b_in, decay_logit, W_out, b_out, D_skip, W_down, b_down, W_up, b_up):
        import jax, jax.numpy as jnp
        import numpy as np
        D_MODEL = 512
        SSM_RANK = 8
        FFN_RANK = D_MODEL // 64
        EPS = 1e-05

        def _layernorm(x, gamma, beta):
            mu = jnp.mean(x, axis=-1, keepdims=True)
            var = jnp.var(x, axis=-1, keepdims=True)
            return (x - mu) * jax.lax.rsqrt(var + EPS) * gamma + beta

        def _ssm_scan(u, decay):
            a = jnp.broadcast_to(decay, u.shape)

            def combine(e1, e2):
                a1, b1 = e1
                a2, b2 = e2
                return (a1 * a2, a2 * b1 + b2)
            _, h = jax.lax.associative_scan(combine, (a, u), axis=1)
            return h
        xn = _layernorm(x, ln_gamma, ln_beta)
        u = jnp.einsum('bsd,dr->bsr', xn, W_in) + b_in
        decay = jax.nn.sigmoid(decay_logit)
        h = _ssm_scan(u, decay)
        x_ar = jnp.einsum('bsr,rd->bsd', h, W_out) + b_out + xn * D_skip
        x = x + x_ar
        xn2 = _layernorm(x, ln_gamma, ln_beta)
        hf = jax.nn.relu(jnp.einsum('bsd,dr->bsr', xn2, W_down) + b_down)
        x_ffn = jnp.einsum('bsr,rd->bsd', hf, W_up) + b_up
        return x + x_ffn

    def _L0_ffn_ref(x, W1, W2, W3):
        import jax, jax.numpy as jnp
        import numpy as np
        B, S, D, H = (4, 512, 512, 2048)

        def fwht(x):
            orig_shape = x.shape
            n = orig_shape[-1]
            x = x.reshape(-1, n)
            h = 1
            while h < n:
                xb = x.reshape(-1, n // (2 * h), 2, h)
                a = xb[:, :, 0, :]
                b = xb[:, :, 1, :]
                x = jnp.stack([a + b, a - b], axis=2).reshape(-1, n)
                h *= 2
            scale = jnp.asarray(1.0 / np.sqrt(n), dtype=x.dtype)
            return (x * scale).reshape(orig_shape)
        up_gate = jnp.einsum('bsd,hd->bsh', x, W1)
        up_lin = jnp.einsum('bsd,hd->bsh', x, W3)
        hidden = jax.nn.silu(up_gate) * up_lin
        hidden = fwht(hidden)
        out = jnp.einsum('bsh,dh->bsd', hidden, W2)
        return out

    def _L1_attn_ref(x, W_qkv, b_qkv, W_out, b_out):
        import jax, jax.numpy as jnp
        import numpy as np
        D_MODEL = 512
        N_HEADS = 16
        HEAD_DIM = D_MODEL // N_HEADS
        b, l, d = x.shape
        h, e = (N_HEADS, HEAD_DIM)
        qkv = x @ W_qkv.T + b_qkv
        q, k, v = jnp.split(qkv, 3, axis=-1)
        q = q.reshape(b, l, h, e)
        k = k.reshape(b, l, h, e)
        v = v.reshape(b, l, h, e)
        scale = 1.0 / jnp.sqrt(jnp.float32(e))
        scores = jnp.einsum('bqhe,bkhe->bhqk', q, k) * scale
        causal = jnp.tril(jnp.ones((l, l), dtype=bool))
        scores = jnp.where(causal[None, None], scores, -jnp.inf)
        attn = jax.nn.softmax(scores, axis=-1)
        out = jnp.einsum('bhqk,bkhe->bqhe', attn, v)
        out = out.reshape(b, l, d)
        out = out @ W_out.T + b_out
        return out

    def _L1_ffn_ref(x, w_gate, w_up, w_down):
        import jax, jax.numpy as jnp
        import numpy as np

        def _sparsify_2to4(h):
            B, S, I = h.shape
            g = h.reshape(B, S, I // 4, 4)
            a = jnp.abs(g)
            _, idx = jax.lax.top_k(a, 2)
            pos = jnp.arange(4)
            mask = (pos == idx[..., 0:1]) | (pos == idx[..., 1:2])
            return (g * mask.astype(g.dtype)).reshape(B, S, I)
        h = jax.nn.silu(jnp.einsum('bsh,hi->bsi', x, w_gate)) * jnp.einsum('bsh,hi->bsi', x, w_up)
        h_sparse = _sparsify_2to4(h)
        return jnp.einsum('bsi,ih->bsh', h_sparse, w_down)
    x = L0_attn_x
    xn = _layernorm(x, axis=-1)
    x = x + _L0_attn_ref(xn, L0_attn_ln_gamma, L0_attn_ln_beta, L0_attn_W_in, L0_attn_b_in, L0_attn_decay_logit, L0_attn_W_out, L0_attn_b_out, L0_attn_D_skip, L0_attn_W_down, L0_attn_b_down, L0_attn_W_up, L0_attn_b_up) + _L0_ffn_ref(xn, L0_ffn_W1, L0_ffn_W2, L0_ffn_W3)
    xn = _layernorm(x, axis=-1)
    x = x + _L1_attn_ref(xn, L1_attn_W_qkv, L1_attn_b_qkv, L1_attn_W_out, L1_attn_b_out) + _L1_ffn_ref(xn, L1_ffn_w_gate, L1_ffn_w_up, L1_ffn_w_down)
    return x

_drawn_inputs = setup_inputs


def setup_inputs(seed=0):
    import zlib

    import numpy as np

    out = dict(_drawn_inputs(seed))
    spreads = {'L0_attn_ln_gamma': (1.0, 0.2),
     'L0_attn_ln_beta': (0.0, 0.1),
     'L0_attn_b_in': (0.0, 0.1),
     'L0_attn_b_out': (0.0, 0.1),
     'L0_attn_b_down': (0.0, 0.8),
     'L0_attn_b_up': (0.0, 0.1)}
    factors = {'L0_attn_W_down': 8.0, 'L0_attn_W_up': 8.0, 'L1_attn_b_qkv': 8.0, 'L1_attn_b_out': 5.973}
    for name, (base, spread) in spreads.items():
        noise = np.random.default_rng([zlib.crc32(name.encode()), seed]).standard_normal(out[name].shape)
        drawn = base * np.exp(spread * noise) if base else spread * noise
        out[name] = jnp.asarray(drawn.astype(out[name].dtype))
    for name, factor in factors.items():
        out[name] = (out[name] * factor).astype(out[name].dtype)
    return out
```

```python
from contextlib import ExitStack

import concourse.bass as bass
from concourse import mybir

F32 = mybir.dt.float32
F32R = mybir.dt.float32r
BF16 = mybir.dt.bfloat16
ALU = mybir.AluOpType
ACT = mybir.ActivationFunctionType
AX_X = mybir.AxisListType.X

P = 128
B, S, D = 2, 1024, 512
T = B * S
NT = T // P
KD = D // P
HID = 2048
NC = 4
NG = HID // (NC * P)
W = 512
TT = T // W
HEADS, E = 16, 32
EPS = 1e-5


def alloc(nc, ctx):
    sems = []

    def sb(name, shape, dt=F32):
        return ctx.enter_context(nc.sbuf_tensor(name, shape, dt))

    def ps(name, shape, dt=F32):
        return ctx.enter_context(nc.psum_tensor(name, shape, dt))

    def sem(name):
        sems.append(nc.alloc_semaphore(name))
        return sems[-1]

    ctx.callback(lambda: sems and nc.clear_and_free_semaphores(sems))
    return sb, ps, sem


def phase(nc, program, *args):
    program(nc, *args)
    nc.all_engine_barrier()


def feed_forward(nc, tag, wgu, wd, x_hi, x_lo, res, sparse):
    UC = NC * TT
    with ExitStack() as ctx:
        sb, ps, sem = alloc(nc, ctx)
        raw_gu = sb(f"{tag}_raw_gu", [P, 2, 2, KD, P])
        raw_d = sb(f"{tag}_raw_d", [P, 2, D])
        gu_hi = sb(f"{tag}_gu_hi", [P, NC, 2, KD, P], F32R)
        gu_lo = sb(f"{tag}_gu_lo", [P, NC, 2, KD, P], F32R)
        d_hi = sb(f"{tag}_d_hi", [P, NC, D], F32R)
        d_lo = sb(f"{tag}_d_lo", [P, NC, D], F32R)
        hid = sb(f"{tag}_hid", [P, 2, NC, W])
        h_hi = sb(f"{tag}_h_hi", [P, NC, W], F32R)
        h_lo = sb(f"{tag}_h_lo", [P, NC, W], F32R)
        if sparse:
            mag = sb(f"{tag}_mag", [P, 2, W])
            top = sb(f"{tag}_top", [P, 2, W])
            low = sb(f"{tag}_low", [P, 2, W])
            first = sb(f"{tag}_first", [P, 2, W], BF16)
            both = sb(f"{tag}_both", [P, 2, W], BF16)
            vote = sb(f"{tag}_vote", [P, 2, W], BF16)
        one = sb(f"{tag}_one", [P, 1])
        p_gate = ps(f"{tag}_p_gate", [P, 2, W])
        p_up = ps(f"{tag}_p_up", [P, 2, W])
        p_out = ps(f"{tag}_p_out", [P, W // P, D])

        gu_loaded = [sem(f"{tag}_gu_loaded{i}") for i in range(2)]
        d_loaded = [sem(f"{tag}_d_loaded{i}") for i in range(2)]
        gu_rounded, gu_split = sem(f"{tag}_gu_rounded"), sem(f"{tag}_gu_split")
        d_rounded, d_split = sem(f"{tag}_d_rounded"), sem(f"{tag}_d_split")
        gate_done, up_done = sem(f"{tag}_gate_done"), sem(f"{tag}_up_done")
        silu_done, hid_done = sem(f"{tag}_silu_done"), sem(f"{tag}_hid_done")
        mag_done, choice = sem(f"{tag}_mag_done"), sem(f"{tag}_choice")
        hi_done, lo_done = sem(f"{tag}_hi_done"), sem(f"{tag}_lo_done")
        out_done, added = sem(f"{tag}_out_done"), sem(f"{tag}_added")
        one_set = sem(f"{tag}_one_set")
        CH = 17

        block = ctx.enter_context(nc.Block())

        @block.sync
        def _(sp):
            def load_gu(g, c, first_group):
                if not (first_group and c < 2):
                    sp.wait_ge(gu_split, NC * g + c - 1)
                sp.dma_start(raw_gu[:, c % 2], wgu[g, c]).then_inc(gu_loaded[c % 2], 16)

            def load_d(g, c, first_group):
                if not (first_group and c < 2):
                    sp.wait_ge(d_split, NC * g + c - 1)
                sp.dma_start(raw_d[:, c % 2], wd[g, c]).then_inc(d_loaded[c % 2], 16)

            for c in range(NC):
                load_gu(0, c, True)
                load_d(0, c, True)
            with sp.Fori(1, NG) as g:
                for c in range(NC):
                    load_gu(g, c, False)
                for c in range(NC):
                    load_d(g, c, False)

        @block.gpsimd
        def _(pool):
            def group(g, first_group=False):
                for c in range(NC):
                    n = NC * g + c
                    pool.wait_ge(gu_loaded[c % 2], 16 * (2 * g + c // 2 + 1))
                    if not first_group:
                        pool.wait_ge(up_done, UC * g - NC + c + 1)
                    pool.tensor_tensor(gu_hi[:, c].rearrange("p j k m -> p (j k m)"),
                                       raw_gu[:, c % 2].rearrange("p j k m -> p (j k m)"),
                                       one[:, :].to_broadcast([P, 2 * KD * P]), ALU.mult).then_inc(gu_rounded, 1)
                    pool.wait_ge(gu_rounded, n + 1)
                    pool.tensor_tensor(gu_lo[:, c], raw_gu[:, c % 2], gu_hi[:, c].bitcast(F32),
                                       ALU.subtract).then_inc(gu_split, 1)
                    if first_group:
                        down_piece(g, c, n)
                if not first_group:
                    pool.wait_ge(out_done, TT * g)
                    for c in range(NC):
                        down_piece(g, c, NC * g + c)

            def down_piece(g, c, n):
                pool.wait_ge(d_loaded[c % 2], 16 * (2 * g + c // 2 + 1))
                pool.tensor_tensor(d_hi[:, c], raw_d[:, c % 2], one[:, :].to_broadcast([P, D]),
                                   ALU.mult).then_inc(d_rounded, 1)
                pool.wait_ge(d_rounded, n + 1)
                pool.tensor_tensor(d_lo[:, c], raw_d[:, c % 2], d_hi[:, c].bitcast(F32),
                                   ALU.subtract).then_inc(d_split, 1)

            pool.memset(one[:], 1.0).then_inc(one_set, 1)
            pool.wait_ge(one_set, 1)
            group(0, True)
            with pool.Fori(1, NG) as g:
                group(g)

        @block.tensor
        def _(pe):
            def hidden(g, t, first_group):
                for c in range(NC):
                    n = UC * g + NC * t + c
                    if t == 0:
                        pe.wait_ge(gu_split, NC * g + c + 1)
                    if not (first_group and t == 0 and c < 2):
                        pe.wait_ge(hid_done, n - 1)
                    for j, (acc, done) in enumerate(((p_gate, gate_done), (p_up, up_done))):
                        for k in range(KD):
                            xs = slice(t * W, (t + 1) * W)
                            pe.matmul(acc[:, c % 2], gu_hi[:, c, j, k], x_hi[:, k, xs], start=(k == 0), stop=False)
                            pe.matmul(acc[:, c % 2], gu_hi[:, c, j, k], x_lo[:, k, xs], start=False, stop=False)
                            mm = pe.matmul(acc[:, c % 2], gu_lo[:, c, j, k], x_hi[:, k, xs], start=False,
                                           stop=(k == KD - 1))
                        mm.then_inc(done, 1)

            def output(u, g, first_unit):
                pe.wait_ge(d_split, NC * g + NC)
                if not first_unit:
                    pe.wait_ge(added, (W // P) * u)
                for c in range(NC):
                    pe.wait_ge(lo_done, NC * u + c + 1)
                    for j in range(W // P):
                        rows = slice(j * P, (j + 1) * P)
                        pe.matmul(p_out[:, j], h_hi[:, c, rows], d_hi[:, c], start=(c == 0), stop=False)
                        pe.matmul(p_out[:, j], h_hi[:, c, rows], d_lo[:, c], start=False, stop=False)
                        mm = pe.matmul(p_out[:, j], h_lo[:, c, rows], d_hi[:, c], start=False, stop=(c == NC - 1))
                mm.then_inc(out_done, 1)

            def group(g, first_group=False):
                for t in range(TT):
                    hidden(g, t, first_group)
                    if not (first_group and t == 0):
                        gp = g if t else g - 1
                        output(TT * g + t - 1, gp, first_group and t == 1)

            group(0, True)
            with pe.Fori(1, NG) as g:
                group(g)
            output(TT * NG - 1, NG - 1, False)

        @block.scalar
        def _(act):
            def unit(g, t, first_group):
                u = TT * g + t
                s = t % 2
                for c in range(NC):
                    n = NC * u + c
                    act.wait_ge(gate_done, n + 1)
                    if not (first_group and t < 2):
                        act.wait_ge(lo_done, n - 2 * NC + 1)
                    act.activation(hid[:, s, c], p_gate[:, c % 2], ACT.Silu).then_inc(silu_done, 1)
                    if sparse:
                        act.wait_ge(hid_done, n + 1)
                        if c >= 2:
                            act.wait_ge(choice, CH * u + 3)
                        elif not (first_group and t == 0):
                            act.wait_ge(choice, CH * (u - 1) + 6)
                        act.activation(mag[:, c % 2], hid[:, s, c], ACT.Abs).then_inc(mag_done, 1)
                for c in range(NC):
                    n = NC * u + c
                    if sparse:
                        act.wait_ge(choice, CH * u + CH - NC + c + 1)
                    else:
                        act.wait_ge(hid_done, n + 1)
                    if c == 0 and not (first_group and t == 0):
                        act.wait_ge(out_done, u)
                    act.activation(h_hi[:, c], hid[:, s, c], ACT.Copy).then_inc(hi_done, 1)

            def group(g, first_group=False):
                for t in range(TT):
                    unit(g, t, first_group)

            group(0, True)
            with act.Fori(1, NG) as g:
                group(g)

        @block.vector
        def _(dve):
            def unit(g, t, first_group):
                u = TT * g + t
                s = t % 2
                ch = CH * u

                def compare(pair):
                    a, b = mag[:, 0], mag[:, 1]
                    dve.wait_ge(mag_done, NC * u + 2 * pair + 2)
                    if pair == 0 and not (first_group and t == 0):
                        dve.wait_ge(choice, ch)
                    dve.tensor_tensor(top[:, pair], a, b, ALU.max).then_inc(choice, 1)
                    dve.tensor_tensor(low[:, pair], a, b, ALU.min).then_inc(choice, 1)
                    dve.tensor_tensor(first[:, pair], a, b, ALU.is_ge).then_inc(choice, 1)

                def choose():
                    dve.wait_ge(choice, ch + 6)
                    dve.tensor_tensor(both[:, 0], low[:, 0], top[:, 1], ALU.is_ge).then_inc(choice, 1)
                    dve.tensor_tensor(both[:, 1], low[:, 1], top[:, 0], ALU.is_gt).then_inc(choice, 1)
                    dve.wait_ge(choice, ch + 8)
                    lead = both[:, 0]
                    dve.tensor_tensor(lead, both[:, 0], both[:, 1], ALU.subtract).then_inc(choice, 1)
                    dve.wait_ge(choice, ch + 9)
                    dve.tensor_tensor(vote[:, 0], first[:, 0], lead, ALU.add).then_inc(choice, 1)
                    dve.tensor_tensor(vote[:, 1], first[:, 1], lead, ALU.subtract).then_inc(choice, 1)
                    dve.wait_ge(choice, ch + 11)
                    dve.tensor_tensor(first[:, 0], first[:, 0], lead, ALU.subtract).then_inc(choice, 1)
                    dve.tensor_tensor(first[:, 1], first[:, 1], lead, ALU.add).then_inc(choice, 1)
                    dve.wait_ge(choice, ch + 13)
                    for c, (votes, op, bound) in enumerate(((vote[:, 0], ALU.is_ge, 1.0), (first[:, 0], ALU.is_le, 0.0),
                                                            (vote[:, 1], ALU.is_ge, 1.0), (first[:, 1], ALU.is_le, 0.0))):
                        dve.scalar_tensor_tensor(hid[:, s, c], votes, bound, hid[:, s, c], op,
                                                 ALU.mult).then_inc(choice, 1)

                for c in range(NC):
                    n = NC * u + c
                    dve.wait_ge(silu_done, n + 1)
                    dve.wait_ge(up_done, n + 1)
                    dve.tensor_tensor(hid[:, s, c], hid[:, s, c], p_up[:, c % 2], ALU.mult).then_inc(hid_done, 1)
                    if sparse and c % 2:
                        compare(c // 2)
                if sparse:
                    choose()
                for c in range(NC):
                    dve.wait_ge(hi_done, NC * u + c + 1)
                    dve.tensor_tensor(h_lo[:, c], hid[:, s, c], h_hi[:, c].bitcast(F32),
                                      ALU.subtract).then_inc(lo_done, 1)

            def add_output(u, t):
                dve.wait_ge(out_done, u + 1)
                for j in range(W // P):
                    r = res[:, t * (W // P) + j]
                    dve.tensor_tensor(r, r, p_out[:, j], ALU.add).then_inc(added, 1)

            def group(g, first_group=False):
                for t in range(TT):
                    unit(g, t, first_group)
                    if not (first_group and t == 0):
                        add_output(TT * g + t - 1, (t - 1) % TT)

            group(0, True)
            with dve.Fori(1, NG) as g:
                group(g)
            add_output(TT * NG - 1, TT - 1)


def norm_steps(nc, ctx, tag, src, dst):
    sb, _, sem = alloc(nc, ctx)
    Q = NT // 4
    stats = sb(f"{tag}_stats", [P, NT, 6])
    mv = sb(f"{tag}_mv", [P, NT, 2])
    var = sb(f"{tag}_var", [P, NT])
    sd = sb(f"{tag}_sd", [P, NT])
    rstd = sb(f"{tag}_rstd", [P, NT])
    t1 = sb(f"{tag}_t1", [P, NT])
    stat, step, sd_done = sem(f"{tag}_stat"), sem(f"{tag}_step"), sem(f"{tag}_sd_done")
    normed, var_done = sem(f"{tag}_normed"), sem(f"{tag}_var_done")
    NS = 5

    def vec_stats(dve, q):
        for i in range(Q * q, Q * q + Q):
            dve.bn_stats(stats[:, i], src[:, i]).then_inc(stat, 1)
        for i in range(Q * q, Q * q + Q):
            dve.wait_ge(stat, 2 * Q * q + i - Q * q + 1)
            dve.bn_aggr(mv[:, i], stats[:, i]).then_inc(stat, 1)
        dve.wait_ge(stat, 2 * Q * (q + 1))
        a = slice(Q * q, Q * q + Q)
        dve.tensor_scalar(var[:, a], mv[:, a, 1], EPS, None, ALU.add).then_inc(var_done, 1)

    def act_sd(act, q):
        a = slice(Q * q, Q * q + Q)
        act.wait_ge(var_done, q + 1)
        act.activation(sd[:, a], var[:, a], ACT.Sqrt).then_inc(sd_done, 1)

    def vec_norm(dve, q):
        a = slice(Q * q, Q * q + Q)
        s = NS * q
        dve.wait_ge(sd_done, q + 1)
        dve.reciprocal(rstd[:, a], sd[:, a]).then_inc(step, 1)
        dve.wait_ge(step, s + 1)
        dve.tensor_tensor(t1[:, a], rstd[:, a], rstd[:, a], ALU.mult).then_inc(step, 1)
        dve.wait_ge(step, s + 2)
        dve.tensor_tensor(t1[:, a], t1[:, a], var[:, a], ALU.mult).then_inc(step, 1)
        dve.wait_ge(step, s + 3)
        dve.tensor_scalar(t1[:, a], t1[:, a], -0.5, 1.5, ALU.mult, ALU.add).then_inc(step, 1)
        dve.wait_ge(step, s + 4)
        dve.tensor_tensor(rstd[:, a], rstd[:, a], t1[:, a], ALU.mult).then_inc(step, 1)
        dve.wait_ge(step, s + 5)
        for i in range(Q * q, Q * q + Q):
            dve.tensor_scalar(dst[:, i], src[:, i], mv[:, i, 0:1], rstd[:, i:i + 1], ALU.subtract,
                              ALU.mult).then_inc(normed, 1)

    return vec_stats, act_sd, vec_norm, normed


def turn_steps(nc, ctx, tag, src, ident, have, banks):
    _, _, sem = alloc(nc, ctx)
    turned, emptied = sem(f"{tag}_turned"), sem(f"{tag}_emptied")
    NB = banks.shape[1]

    def pe_turn(pe, q):
        pe.wait_ge(have, (NT // 4) * (q + 1))
        for k in range(KD):
            m = KD * q + k
            if m >= NB:
                pe.wait_ge(emptied, m - NB + 1)
            for j in range(W // P):
                mm = pe.transpose(banks[:, m % NB, j * P:(j + 1) * P],
                                  src[:, (NT // 4) * q + j, k * P:(k + 1) * P], ident[:, :])
            mm.then_inc(turned, 1)

    return pe_turn, turned, emptied


def split_turned(nc, ctx, tag, banks, turned, emptied, x_hi, x_lo):
    _, _, sem = alloc(nc, ctx)
    rounded = sem(f"{tag}_rounded")
    NB = banks.shape[1]

    def act_hi(act, q):
        for k in range(KD):
            m = KD * q + k
            act.wait_ge(turned, m + 1)
            act.activation(x_hi[:, k, q * W:(q + 1) * W], banks[:, m % NB], ACT.Copy).then_inc(rounded, 1)

    def vec_lo(dve, q):
        for k in range(KD):
            m = KD * q + k
            dve.wait_ge(rounded, m + 1)
            cols = slice(q * W, (q + 1) * W)
            dve.tensor_tensor(x_lo[:, k, cols], banks[:, m % NB], x_hi[:, k, cols].bitcast(F32),
                              ALU.subtract).then_inc(emptied, 1)

    return act_hi, vec_lo


def prepare(nc, x, w2t, signs, eye, w2f, ident, res, n1, x_hi, x_lo):
    NCH = HID // P
    with ExitStack() as ctx:
        sb, ps, sem = alloc(nc, ctx)
        w2 = sb("w2", [P, NCH, D])
        rot = sb("rot", [P, NCH, D])
        sign = sb("sign", [P, 2, P])
        banks = ps("banks", [P, 4, W])
        p_rot = ps("p_rot", [P, 4, D])
        x_loaded = [sem(f"x_loaded{q}") for q in range(4)]
        w2_loaded = [sem(f"w2_loaded{q}") for q in range(4)]
        sign_loaded, eye_loaded = sem("sign_loaded"), sem("eye_loaded")
        rot_done, rot_copied, flown, w2f_stored = sem("rot_done"), sem("rot_copied"), sem("flown"), sem("w2f_stored")
        vec_stats, act_sd, vec_norm, normed = norm_steps(nc, ctx, "n1", res, n1)
        pe_turn, turned, emptied = turn_steps(nc, ctx, "t1", n1, ident, normed, banks)
        act_hi, vec_lo = split_turned(nc, ctx, "s1", banks, turned, emptied, x_hi, x_lo)
        block = ctx.enter_context(nc.Block())

        @block.sync
        def _(sp):
            xt = x.rearrange("(n p) d -> p n d", p=P)
            w2c = w2t.rearrange("(n p) d -> p n d", p=P)
            sp.dma_start(ident[:], eye).then_inc(eye_loaded, 16)
            for q in range(4):
                sp.dma_start(res[:, 4 * q:4 * q + 4], xt[:, 4 * q:4 * q + 4]).then_inc(x_loaded[q], 16)
            sp.dma_start(sign[:], signs).then_inc(sign_loaded, 16)
            for q in range(4):
                sp.dma_start(w2[:, 4 * q:4 * q + 4], w2c[:, 4 * q:4 * q + 4]).then_inc(w2_loaded[q], 16)
            out = w2f.rearrange("n p d -> p n d")
            for h in range(2):
                sp.wait_ge(flown, 4 + h + 1)
                sp.dma_start(out[:, 8 * h:8 * h + 8], w2[:, 8 * h:8 * h + 8]).then_inc(w2f_stored, 16)
            sp.wait_ge(w2f_stored, 32)

        @block.tensor
        def _(pe):
            pe.wait_ge(eye_loaded, 16)
            pe_turn(pe, 0)
            pe_turn(pe, 1)
            pe_turn(pe, 2)
            pe_turn(pe, 3)
            pe.wait_ge(sign_loaded, 16)
            for a in range(0, NCH, 2):
                if a % 4 == 0:
                    pe.wait_ge(w2_loaded[a // 4], 16)
                for s in range(2):
                    n = a + s
                    if n >= 4:
                        pe.wait_ge(rot_copied, n - 3)
                    pe.matmul(p_rot[:, n % 4], sign[:, 0], w2[:, a], start=True, stop=False)
                    pe.matmul(p_rot[:, n % 4], sign[:, s], w2[:, a + 1], start=False, stop=True).then_inc(rot_done, 1)

        @block.scalar
        def _(act):
            for q in range(4):
                act_sd(act, q)
                if q:
                    act_hi(act, q - 1)
            act_hi(act, 3)
            for n in range(NCH):
                act.wait_ge(rot_done, n + 1)
                act.activation(rot[:, n], p_rot[:, n % 4], ACT.Copy, scale=float(1.0 / HID ** 0.5)).then_inc(rot_copied, 1)

        @block.vector
        def _(dve):
            dve.wait_ge(x_loaded[0], 16)
            vec_stats(dve, 0)
            for q in range(4):
                if q < 3:
                    dve.wait_ge(x_loaded[q + 1], 16)
                    vec_stats(dve, q + 1)
                vec_norm(dve, q)
                if q:
                    vec_lo(dve, q - 1)
            vec_lo(dve, 3)
            here, there = rot, w2
            dve.wait_ge(rot_copied, NCH)
            for s in range(1, 4):
                lo = 2 ** s
                a, b = (t[:].rearrange("p (h two l) d -> p h two (l d)", two=2, l=lo) for t in (here, there))
                if s > 1:
                    dve.wait_ge(flown, 2 * (s - 1))
                for j, op in enumerate((ALU.add, ALU.subtract)):
                    dve.tensor_tensor(b[:, :, j], a[:, :, 0], a[:, :, 1], op).then_inc(flown, 1)
                here, there = there, here
            assert here is w2


def state_space_branch(nc, cols, rank, rows, ident, res, n1, tag="ssm"):
    R = rank.shape[0]
    Q = NT // 4
    with ExitStack() as ctx:
        sb, ps, sem = alloc(nc, ctx)
        z = sb("z", [P, NT, D])
        zT = sb("zT", [P, 2, KD, W])
        col = sb("col", [P, cols.shape[1]])
        row = sb("row", [P, 5, D])
        low = sb("low", [R, T])
        rk = sb("rk", [R, rank.shape[1]])
        decay = sb("decay", [R, 1])
        ones = sb("ones", [R, S])
        gamma, beta = col[:, 0:KD], col[:, KD:2 * KD]
        w_in = col[:, 2 * KD:2 * KD + KD * R].rearrange("p (k r) -> p k r", k=KD)
        w_down = col[:, 2 * KD + KD * R:].rearrange("p (k r) -> p k r", k=KD)
        g_row, b_row, skip_row, bout_row, bup_row = (row[:, i] for i in range(5))
        b_in, logit, b_down = (rk[:, i:i + 1] for i in range(3))
        w_out, w_up = rk[:, 3:3 + D], rk[:, 3 + D:3 + 2 * D]
        banks = ps("ssm_banks", [P, 4, W])
        p_low = ps("p_low", [R, 1, W])
        p_wide = ps("p_wide", [P, 3, D])

        loaded, row_step, decay_step = sem("loaded"), sem("row_step"), sem("decay_step")
        res_biased, n1_biased, skipped, with_skip = sem("res_biased"), sem("n1_biased"), sem("skipped"), sem("with_skip")
        low_done, low_copied, scanned = sem("low_done"), sem("low_copied"), sem("scanned")
        wide_done, wide_added, res_x1 = sem("wide_done"), sem("wide_added"), sem("res_x1")
        st1, sd1, no1, normed1 = norm_steps(nc, ctx, "n2", n1, z)
        st2, sd2, no2, normed2 = norm_steps(nc, ctx, "n3", n1, z)
        turn1, turned1, shifted1 = turn_steps(nc, ctx, "t2", z, ident, normed1, banks)
        turn2, turned2, shifted2 = turn_steps(nc, ctx, "t3", z, ident, normed2, banks)
        block = ctx.enter_context(nc.Block())

        @block.sync
        def _(sp):
            sp.dma_start(row[:].rearrange("p a d -> p (a d)"), rows.to_broadcast([P, 5 * D])).then_inc(loaded, 16)
            sp.dma_start(col[:], cols).then_inc(loaded, 16)
            sp.dma_start(rk[:], rank).then_inc(loaded, 16)

        @block.gpsimd
        def _(pool):
            pool.memset(ones[:], 1.0).then_inc(decay_step, 1)
            pool.wait_ge(loaded, 48)
            pool.tensor_tensor(b_row, b_row, skip_row, ALU.mult).then_inc(row_step, 1)
            pool.tensor_tensor(g_row, g_row, skip_row, ALU.mult).then_inc(row_step, 1)
            pool.wait_ge(row_step, 1)
            pool.tensor_tensor(b_row, b_row, bout_row, ALU.add).then_inc(row_step, 1)
            for i in range(NT):
                if i == 0:
                    pool.wait_ge(row_step, 3)
                if i % Q == 0:
                    pool.wait_ge(turned1, KD * (i // Q + 1))
                pool.tensor_tensor(n1[:, i], n1[:, i], b_row, ALU.add).then_inc(n1_biased, 1)
                pool.tensor_tensor(z[:, i], z[:, i], g_row, ALU.mult).then_inc(skipped, 1)
            for i in range(NT):
                pool.tensor_tensor(res[:, i], res[:, i], bup_row, ALU.add).then_inc(res_biased, 1)
                pool.wait_ge(res_biased, i + 1)
                pool.wait_ge(wide_added, i + 1)
                pool.tensor_tensor(res[:, i], res[:, i], n1[:, i], ALU.add).then_inc(res_x1, 1)

        @block.tensor
        def _(pe):
            def low_rank(w, shifted, q, n):
                pe.wait_ge(shifted, KD * (q + 1))
                if n:
                    pe.wait_ge(low_copied, n)
                for k in range(KD):
                    mm = pe.matmul(p_low[:, 0], w[:, k], zT[:, n % 2, k], start=(k == 0), stop=(k == KD - 1))
                mm.then_inc(low_done, 1)

            def widen(w, i, n):
                if n >= 3:
                    pe.wait_ge(wide_added, n - 2)
                pe.matmul(p_wide[:, n % 3], low[:, i * P:(i + 1) * P], w, start=True, stop=True).then_inc(wide_done, 1)

            pe.wait_ge(loaded, 48)
            for q in range(4):
                turn1(pe, q)
                if q:
                    low_rank(w_in, shifted1, q - 1, q - 1)
                if q == 3:
                    pe.wait_ge(scanned, 1)
                    for i in range(NT // 2):
                        widen(w_out, i, i)
            low_rank(w_in, shifted1, 3, 3)
            pe.wait_ge(scanned, 2)
            for i in range(NT // 2, NT):
                widen(w_out, i, i)
            pe.wait_ge(shifted1, 4 * KD)
            for q in range(4):
                turn2(pe, q)
                if q:
                    low_rank(w_down, shifted2, q - 1, 4 + q - 1)
                    pe.wait_ge(low_copied, 4 + q)
                    for i in range(Q * (q - 1), Q * q):
                        widen(w_up, i, NT + i)
            low_rank(w_down, shifted2, 3, 7)
            pe.wait_ge(low_copied, 8)
            for i in range(Q * 3, Q * 4):
                widen(w_up, i, NT + i)

        @block.scalar
        def _(act):
            def shift(q, turned, shifted, again):
                for k in range(KD):
                    m = KD * q + k
                    act.wait_ge(turned, m + 1)
                    if k == 0 and (again or q >= 2):
                        act.wait_ge(low_done, 4 * again + q - 1)
                    act.activation(zT[:, q % 2, k], banks[:, m % 4], ACT.Identity, bias=beta[:, k:k + 1],
                                   scale=gamma[:, k:k + 1]).then_inc(shifted, 1)

            def low_copy(q, n, func, bias):
                act.wait_ge(low_done, n + 1)
                if func == ACT.Relu and q == 0:
                    act.wait_ge(wide_done, NT)
                act.activation(low[:, q * W:(q + 1) * W], p_low[:, 0], func, bias=bias).then_inc(low_copied, 1)

            act.wait_ge(loaded, 48)
            act.activation(decay[:], logit, ACT.Sigmoid).then_inc(decay_step, 1)
            for q in range(4):
                sd1(act, q)
                if q:
                    shift(q - 1, turned1, shifted1, False)
                if q > 1:
                    low_copy(q - 2, q - 2, ACT.Identity, b_in)
            shift(3, turned1, shifted1, False)
            low_copy(2, 2, ACT.Identity, b_in)
            low_copy(3, 3, ACT.Identity, b_in)
            for q in range(4):
                sd2(act, q)
                if q:
                    shift(q - 1, turned2, shifted2, True)
                if q > 1:
                    low_copy(q - 2, 4 + q - 2, ACT.Relu, b_down)
            shift(3, turned2, shifted2, True)
            low_copy(2, 6, ACT.Relu, b_down)
            low_copy(3, 7, ACT.Relu, b_down)

        @block.vector
        def _(dve):
            def scan(b):
                dve.wait_ge(low_copied, 2 * (b + 1))
                dve.tensor_tensor_scan(low[:, b * S:(b + 1) * S], ones[:], low[:, b * S:(b + 1) * S], 0.0, ALU.mult,
                                       ALU.add).then_inc(scanned, 1)

            def add_skip(q):
                for i in range(Q * q, Q * q + Q):
                    dve.wait_ge(skipped, i + 1)
                    dve.wait_ge(n1_biased, i + 1)
                    dve.tensor_tensor(n1[:, i], n1[:, i], z[:, i], ALU.add).then_inc(with_skip, 1)

            def add_states(q):
                for i in range(Q * q, Q * q + Q):
                    dve.wait_ge(wide_done, i + 1)
                    dve.wait_ge(with_skip, i + 1)
                    dve.tensor_tensor(n1[:, i], n1[:, i], p_wide[:, i % 3], ALU.add).then_inc(wide_added, 1)

            def add_up(q):
                for i in range(Q * q, Q * q + Q):
                    dve.wait_ge(wide_done, NT + i + 1)
                    dve.wait_ge(res_x1, i + 1)
                    dve.tensor_tensor(res[:, i], res[:, i], p_wide[:, (NT + i) % 3], ALU.add).then_inc(wide_added, 1)

            st1(dve, 0)
            for q in range(4):
                if q < 3:
                    st1(dve, q + 1)
                no1(dve, q)
                if q == 0:
                    dve.wait_ge(decay_step, 2)
                    dve.tensor_scalar(ones[:], ones[:], decay[:], None, ALU.mult).then_inc(decay_step, 1)
            dve.wait_ge(decay_step, 3)
            add_skip(0)
            scan(0)
            add_skip(1)
            add_states(0)
            add_states(1)
            add_skip(2)
            add_skip(3)
            scan(1)
            dve.wait_ge(wide_added, Q)
            st2(dve, 0)
            add_states(2)
            add_states(3)
            for q in range(4):
                if q < 3:
                    dve.wait_ge(wide_added, Q * (q + 2))
                    st2(dve, q + 1)
                if q == 0:
                    dve.wait_ge(with_skip, NT)
                no2(dve, q)
                if q > 1:
                    add_up(q - 2)
            add_up(2)
            add_up(3)


def renorm(nc, res, parked, ident, x_hi, x_lo):
    with ExitStack() as ctx:
        sb, ps, sem = alloc(nc, ctx)
        n2 = sb("n2", [P, NT, D])
        banks = ps("banks2", [P, 4, W])
        stored = sem("stored")
        vec_stats, act_sd, vec_norm, normed = norm_steps(nc, ctx, "n4", res, n2)
        pe_turn, turned, emptied = turn_steps(nc, ctx, "t4", n2, ident, normed, banks)
        act_hi, vec_lo = split_turned(nc, ctx, "s4", banks, turned, emptied, x_hi, x_lo)
        block = ctx.enter_context(nc.Block())

        @block.sync
        def _(sp):
            sp.dma_start(parked.rearrange("(n p) d -> p n d", p=P), res[:]).then_inc(stored, 16)
            sp.wait_ge(stored, 16)

        @block.tensor
        def _(pe):
            for q in range(4):
                pe_turn(pe, q)

        @block.scalar
        def _(act):
            for q in range(4):
                act_sd(act, q)
                if q:
                    act_hi(act, q - 1)
            act_hi(act, 3)

        @block.vector
        def _(dve):
            vec_stats(dve, 0)
            for q in range(4):
                if q < 3:
                    vec_stats(dve, q + 1)
                vec_norm(dve, q)
                if q:
                    vec_lo(dve, q - 1)
            vec_lo(dve, 3)


def project_qkv(nc, wqk, wv, qk_bias, qk_scale, x_hi, x_lo, qk_dram, v_dram):
    QUADS = HEADS // 4
    QB = W // P
    QK = 2 * B * 2
    JOBS = QK + B * 2
    BANKS = 6
    with ExitStack() as ctx:
        sb, ps, sem = alloc(nc, ctx)
        raw_w = sb("raw_w", [P, 3, KD, P])
        w_hi = sb("w_hi", [P, 3, KD, P], F32R)
        w_lo = sb("w_lo", [P, 3, KD, P], F32R)
        bias = sb("bias", [P, 2 * QUADS])
        pair_bias = sb("pair_bias", [P, 2])
        scale = sb("scale", [P, 1])
        one = sb("one", [P, 1])
        val = sb("val", [P, 2, W])
        qk = sb("qk", [P, 2, 2, S], F32R)
        v = sb("v_out", [P, B, S // P, 4, 2, E], F32R)
        p_job = ps("p_job", [P, BANKS, W])

        consts, one_set, scale_done = sem("consts"), sem("one_set"), sem("scale_done")
        w_loaded = [sem(f"w_loaded{i}") for i in range(3)]
        w_rounded = [sem(f"w_rounded{i}") for i in range(3)]
        w_split = [sem(f"w_split{i}") for i in range(3)]
        w_biased = [sem(f"w_biased{i}") for i in range(2)]
        job_done, job_used = sem("job_done"), sem("job_used")
        qk_rounded, qk_split, v_rounded, v_split = sem("qk_rounded"), sem("qk_split"), sem("v_rounded"), sem("v_split")
        qk_stored = [sem(f"qk_stored{i}") for i in range(2)]
        v_stored = [sem(f"v_stored{b}") for b in range(B)]
        block = ctx.enter_context(nc.Block())

        def weight_of(m):
            return m // 4 if m < QK else 2

        @block.sync
        def _(sp):
            def load_w(quad, i, first=False):
                if not first:
                    sp.wait_ge(w_split[i], quad)
                src = wv[quad] if i == 2 else wqk[quad, i]
                sp.dma_start(raw_w[:, i], src).then_inc(w_loaded[i], 16)

            def body(it, last):
                if not last:
                    for i in range(3):
                        load_w(it + 1, i)
                for n in range(4):
                    pair = 2 * (n % 2) + n // 2
                    sp.wait_ge(qk_split, QK * it + 2 * n + 2)
                    sp.dma_start(qk_dram[4 * it + pair].rearrange("h p n -> p h n"), qk[:, n % 2].bitcast(F32))\
                        .then_inc(qk_stored[n % 2], 16)
                for b in range(B):
                    sp.wait_ge(v_split, 2 * B * it + 2 * b + 2)
                    sp.dma_start(v_dram[B * it + b], v[:, b].rearrange("p t a h e -> p (t a h e)").bitcast(F32))\
                        .then_inc(v_stored[b], 16)

            load_w(0, 0, True)
            sp.dma_start(bias[:], qk_bias).then_inc(consts, 16)
            sp.dma_start(scale[:], qk_scale).then_inc(consts, 16)
            load_w(0, 1, True)
            load_w(0, 2, True)
            with sp.Fori(0, QUADS - 1) as it:
                body(it, False)
            body(QUADS - 1, True)
            for i in range(2):
                sp.wait_ge(qk_stored[i], 16 * 2 * QUADS)
            for b in range(B):
                sp.wait_ge(v_stored[b], 16 * QUADS)

        @block.gpsimd
        def _(pool):
            def split_w(quad, i, first=False):
                pool.wait_ge(w_loaded[i], 16 * (quad + 1))
                if not first:
                    pool.wait_ge(job_done, JOBS * (quad - 1) + (4 * i + 4 if i < 2 else JOBS))
                pool.tensor_tensor(w_hi[:, i].rearrange("p k m -> p (k m)"), raw_w[:, i].rearrange("p k m -> p (k m)"),
                                   one[:, :].to_broadcast([P, D]), ALU.mult).then_inc(w_rounded[i], 1)
                pool.wait_ge(w_rounded[i], quad + 1)
                pool.tensor_tensor(w_lo[:, i], raw_w[:, i], w_hi[:, i].bitcast(F32), ALU.subtract).then_inc(w_split[i], 1)

            pool.memset(one[:], 1.0).then_inc(one_set, 1)
            pool.wait_ge(one_set, 1)
            for i in range(3):
                split_w(0, i, True)
            with pool.Fori(1, QUADS) as quad:
                for i in range(3):
                    split_w(quad, i)

        @block.tensor
        def _(pe):
            def body(it, first):
                for m in range(JOBS):
                    i = weight_of(m)
                    if m % 4 == 0:
                        pe.wait_ge(w_split[i], it + 1)
                    if not (first and m < BANKS):
                        old, quad = (m - BANKS, it) if m >= BANKS else (m - BANKS + JOBS, it - 1)
                        if old < QK:
                            pe.wait_ge(job_used, QK * quad + old + 1)
                        else:
                            pe.wait_ge(v_split, 2 * B * quad + old - QK + 1)
                    bank = m % BANKS
                    b, part = m % 4 // 2, m % 2
                    t0 = b * S + part * W
                    ways = ((w_hi, x_hi), (w_hi, x_lo), (w_lo, x_hi))
                    if m < QK:
                        for k in range(KD):
                            for y, (w, x) in enumerate(ways):
                                mm = pe.matmul(p_job[:, bank], w[:, i, k], x[:, k, t0:t0 + W], start=(k + y == 0),
                                               stop=(k == KD - 1 and y == 2))
                    else:
                        for tb in range(QB):
                            for k in range(KD):
                                for y, (w, x) in enumerate(ways):
                                    mm = pe.matmul(p_job[:, bank, tb * P:(tb + 1) * P],
                                                   x[:, k, t0 + tb * P:t0 + (tb + 1) * P], w[:, i, k],
                                                   start=(k + y == 0), stop=(k == KD - 1 and y == 2))
                    mm.then_inc(job_done, 1)

            body(0, True)
            with pe.Fori(1, QUADS) as it:
                body(it, False)

        @block.scalar
        def _(act):
            def body(it, first):
                for m in range(JOBS):
                    i = weight_of(m)
                    act.wait_ge(job_done, JOBS * it + m + 1)
                    if m < QK:
                        if m % 4 == 0:
                            act.wait_ge(w_biased[i], it + 1)
                        if not (first and m < 2):
                            act.wait_ge(qk_split, QK * it + m - 1)
                        act.activation(val[:, m % 2], p_job[:, m % BANKS], ACT.Identity, bias=pair_bias[:, i:i + 1],
                                       scale=scale[:, 0:1]).then_inc(job_used, 1)
                        continue
                    b, part = m % 4 // 2, m % 2
                    if not first and part == 0:
                        act.wait_ge(v_stored[b], 16 * it)
                    act.activation(v[:, b, QB * part:QB * part + QB, :, 0, :],
                                   p_job[:, m % BANKS].rearrange("p (t h e) -> p t h e", t=QB, h=4),
                                   ACT.Copy).then_inc(v_rounded, 1)

            act.wait_ge(consts, 32)
            body(0, True)
            with act.Fori(1, QUADS) as it:
                body(it, False)

        @block.vector
        def _(dve):
            def body(it, first):
                for m in range(JOBS):
                    if m in (0, 4):
                        i = m // 4
                        if not first:
                            dve.wait_ge(job_used, QK * (it - 1) + m + 4)
                        dve.tensor_copy(pair_bias[:, i:i + 1], bias[:, bass.ds(2 * it + i, 1)]).then_inc(w_biased[i], 1)
                    b, part = m % 4 // 2, m % 2
                    if m < QK:
                        dve.wait_ge(job_used, QK * it + m + 1)
                        if part == 0 and not (first and m < 4):
                            dve.wait_ge(qk_stored[m // 2 % 2], 16 * (2 * it + m // 4))
                        hi, lo = (qk[:, m // 2 % 2, half, part * W:(part + 1) * W] for half in range(2))
                        dve.tensor_copy(hi, val[:, m % 2]).then_inc(qk_rounded, 1)
                        dve.wait_ge(qk_rounded, QK * it + m + 1)
                        dve.tensor_tensor(lo, val[:, m % 2], hi.bitcast(F32), ALU.subtract).then_inc(qk_split, 1)
                        continue
                    dve.wait_ge(v_rounded, 2 * B * it + m - QK + 1)
                    here = v[:, b, QB * part:QB * part + QB]
                    dve.tensor_tensor(here[:, :, :, 1, :], p_job[:, m % BANKS].rearrange("p (t h e) -> p t h e", t=QB, h=4),
                                      here[:, :, :, 0, :].bitcast(F32), ALU.subtract).then_inc(v_split, 1)

            dve.wait_ge(consts, 32)
            dve.tensor_scalar(bias[:], bias[:], scale[:, 0:1], None, ALU.mult).then_inc(scale_done, 1)
            dve.wait_ge(scale_done, 1)
            body(0, True)
            with dve.Fori(1, QUADS) as it:
                body(it, False)


def attention(nc, masks, ident, qk_dram, v_dram, o_dram, total):
    G = 2
    QB = 4
    QUADS = HEADS // 4
    HB = B * 4
    ROWS = QB * G
    BL = 12
    TB = 3
    PT = 6
    OS = 4
    AHEAD, BEHIND = 2, 1
    ORDER = {
        "tensor": [("weigh", 10, -1), ("weigh", 11, -1), ("turn", 3, 0), ("score", 1, 1), ("turn", 4, 0),
                   ("score", 2, 1), ("turn", 5, 0), ("weigh", 0, 0), ("turn", 6, 0), ("weigh", 1, 0),
                   ("score", 3, 1), ("turn", 7, 0), ("turn", 8, 0), ("score", 4, 1), ("weigh", 2, 0),
                   ("weigh", 3, 0), ("turn", 9, 0), ("score", 5, 1), ("turn", 10, 0), ("weigh", 4, 0),
                   ("weigh", 5, 0), ("score", 6, 1), ("turn", 11, 0), ("weigh", 6, 0), ("turn", 0, 1),
                   ("score", 7, 1), ("weigh", 7, 0), ("turn", 1, 1), ("turn", 2, 1), ("weigh", 8, 0),
                   ("score", 0, 2), ("weigh", 9, 0)],
        "scalar": [("round", 2, 0), ("exp", 0, 1), ("round", 3, 0), ("read_o", 1, -1), ("round", 4, 0),
                   ("round", 5, 0), ("exp", 1, 1), ("exp", 2, 1), ("round", 6, 0), ("round", 7, 0),
                   ("exp", 3, 1), ("round", 8, 0), ("read_o", 0, 0), ("exp", 4, 1), ("round", 9, 0),
                   ("exp", 5, 1), ("round", 10, 0), ("round", 11, 0), ("round", 0, 1), ("exp", 6, 1),
                   ("round", 1, 1), ("exp", 7, 1)],
        "vector": [("rest", 1, 0), ("top", 0, 1), ("rest", 2, 0), ("rest", 3, 0), ("top", 1, 1),
                   ("top", 2, 1), ("rest", 4, 0), ("rest", 5, 0), ("top", 3, 1), ("rest", 6, 0),
                   ("rest", 7, 0), ("top", 4, 1), ("rest", 8, 0), ("top", 5, 1), ("rest", 9, 0),
                   ("top", 6, 1), ("rest", 10, 0), ("rest", 11, 0), ("top", 7, 1), ("rest", 0, 1)],
    }

    with ExitStack() as ctx:
        sb, ps, sem = alloc(nc, ctx)
        stack = sb("stack", [P, 2, 2, 2, S], F32R)
        v = sb("v", [P, B, S // P, 4, 2, E], F32R)
        prob = [sb("prob0", [P, 2, QB, W]), sb("prob1", [P, 2, QB, S])]
        top = sb("row_top", [P, ROWS])
        pt_hi = sb("pt_hi", [P, PT, W], F32R)
        pt_lo = sb("pt_lo", [P, PT, W], F32R)
        o_both = sb("o_both", [2 * E, OS, W])
        mask = sb("mask", [P, 2, P], BF16)
        mask_f = sb("mask_f", [P, 2, P])
        p_score = ps("p_score", [P, 2, S])
        p_turn = ps("p_turn", [P, TB, W])
        p_o = ps("p_o", [P, W])

        mask_loaded, masked = sem("mask_loaded"), sem("masked")
        stacked = [sem(f"stacked{i}") for i in range(2)]
        scored, topped, exped = sem("scored"), sem("topped"), sem("exped")
        turned, rounded, split, weighted = sem("turned"), sem("rounded"), sem("split"), sem("weighted")
        o_read = sem("o_read")
        v_loaded = [sem(f"v_loaded{b}") for b in range(B)]
        o_stored = [sem(f"o_stored{i}") for i in range(OS)]
        STACKS = 8 * 16

        def wait(engine, semaphore, count):
            if not isinstance(count, int) or count > 0:
                engine.wait_ge(semaphore, count)

        def width_of(r):
            return (r + 1) * P

        def place_of(h):
            return h // 4, h // 2 % 2, h % 2

        def block_of(j):
            g, kb = (0, j) if j < QB else (1, j - QB)
            return g, kb, max(0, kb - QB * g) * P

        def run(steps, order):
            def heads(it, hs):
                for h in hs:
                    for step, n, ahead in order:
                        head = h + ahead
                        if isinstance(it, int) and not 0 <= HB * it + head < HB * QUADS:
                            continue
                        steps[step](it + head // HB, head % HB, n)

            heads(0, range(-AHEAD, HB))
            with steps["engine"].Fori(1, QUADS - 1) as it:
                heads(it, range(HB))
            heads(QUADS - 1, range(HB + BEHIND))

        block = ctx.enter_context(nc.Block())

        @block.sync
        def _(sp):
            def load_stack(it, n, first):
                if not (first and n < 2):
                    sp.wait_ge(scored, 2 * ROWS * (4 * it + n - 1))
                here = qk_dram[4 * it + n]
                for a in range(2):
                    for what in range(2):
                        r = 2 * E * what + E * a
                        src = here[:, r:r + E, :]
                        for half in range(2):
                            s = src[half].unsqueeze(0).to_broadcast([2, E, S]) if what == 0 else src
                            sp.dma_start(stack[64 * half:64 * half + 64, n % 2, a, what].bitcast(F32),
                                         s).then_inc(stacked[n % 2], 16)

            def load_v(quad, b, first=False):
                if not first:
                    sp.wait_ge(weighted, HB * BL * quad + (b - 1) * (HB * BL // 2))
                sp.dma_start(v[:, b].rearrange("p t a h e -> p (t a h e)").bitcast(F32),
                             v_dram[B * quad + b]).then_inc(v_loaded[b], 16)

            def store_o(it, h, g):
                b, pr, a = place_of(h)
                sp.wait_ge(o_read, G * (HB * it + h) + g + 1)
                row, t0 = E * (2 * pr + a), b * S + g * W
                sp.dma_start(o_dram[it, :, row:row + E, t0:t0 + W], o_both[:, (G * h + g) % OS])\
                    .then_inc(o_stored[(G * h + g) % OS], 16)

            def body(it, first, last):
                for h in range(HB):
                    for g in range(G):
                        store_o(it, h, g)
                    n = h // 2 + 2
                    if h % 2 == 0 and not (last and n >= 4):
                        load_stack(it + n // 4, n % 4, False)
                    if h == 0 and not first:
                        load_v(it, 1)
                    if h == 4 and not last:
                        load_v(it + 1, 0)

            load_stack(0, 0, True)
            sp.dma_start(mask_f[:], masks).then_inc(mask_loaded, 16)
            load_v(0, 0, True)
            load_stack(0, 1, True)
            load_v(0, 1, True)
            body(0, True, False)
            with sp.Fori(1, QUADS - 1) as it:
                body(it, False, False)
            body(QUADS - 1, False, True)
            for i in range(OS):
                sp.wait_ge(o_stored[i], 16 * (G * HEADS * B // OS))

        @block.tensor
        def _(pe):
            def score(it, h, r):
                pair, a = h // 2, h % 2
                if r == 0 and a == 0:
                    pe.wait_ge(stacked[pair % 2], STACKS * (2 * it + pair // 2 + 1))
                wait(pe, exped, ROWS * (HB * it + h) + r - 1)
                q = stack[:, pair % 2, a, 0, r * P:(r + 1) * P]
                for c0 in range(0, width_of(r), W):
                    c1 = min(width_of(r), c0 + W)
                    pe.matmul(p_score[:, r % 2, c0:c1], q, stack[:, pair % 2, a, 1, c0:c1], start=True,
                              stop=c1 < width_of(r))
                pe.matmul(p_score[:, r % 2, r * P:(r + 1) * P], mask[:, 1], mask[:, 0], start=False,
                          stop=True).then_inc(scored, 1)

            def turn(it, h, j):
                g, kb, c0 = block_of(j)
                if kb == 0:
                    pe.wait_ge(exped, ROWS * (HB * it + h) + QB * (g + 1))
                wait(pe, split, BL * (HB * it + h) + j - TB + 1)
                for i in range(c0 // P, QB):
                    mm = pe.transpose(p_turn[:, (BL * h + j) % TB, i * P:(i + 1) * P],
                                      prob[g][:, h % 2, i, kb * P:(kb + 1) * P], ident[:, :])
                mm.then_inc(turned, 1)

            def weigh(it, h, j):
                b, pr, a = place_of(h)
                g, kb, c0 = block_of(j)
                if j == 0 and h % 4 == 0:
                    pe.wait_ge(v_loaded[b], 16 * (it + 1))
                if kb == 0:
                    wait(pe, o_read, G * (HB * it + h) + g)
                pe.wait_ge(split, BL * (HB * it + h) + j + 1)
                lhs = v[:, b, kb, 2 * pr:2 * pr + 2].rearrange("p a h e -> p (a h e)")
                slot = (BL * h + j) % PT
                pe.matmul(p_o[:, c0:W], lhs, pt_hi[:, slot, c0:W], start=(kb == 0), stop=False)
                pe.matmul(p_o[:, c0:W], lhs, pt_lo[:, slot, c0:W], start=False,
                          stop=(j in (QB - 1, BL - 1))).then_inc(weighted, 1)

            pe.wait_ge(masked, 1)
            run({"engine": pe, "score": score, "turn": turn, "weigh": weigh}, ORDER["tensor"])

        @block.scalar
        def _(act):
            def exp(it, h, r):
                b, pr, a = place_of(h)
                act.wait_ge(topped, ROWS * (HB * it + h) + r + 1)
                wait(act, turned, BL * (HB * it + h - 2) + (r + 1 if r < QB else QB + r + 1))
                sums = total[:, bass.ds(QB * G * 4 * (B * it + b) + 4 * r + 2 * pr + a, 1)]
                act.activation(prob[r // QB][:, h % 2, r % QB, 0:width_of(r)], p_score[:, r % 2, 0:width_of(r)], ACT.Exp,
                               bias=top[:, r:r + 1], accum_out=sums).then_inc(exped, 1)

            def round_block(it, h, j):
                g, kb, c0 = block_of(j)
                act.wait_ge(turned, BL * (HB * it + h) + j + 1)
                wait(act, weighted, BL * (HB * it + h) + j - PT + 1)
                act.activation(pt_hi[:, (BL * h + j) % PT, c0:W], p_turn[:, (BL * h + j) % TB, c0:W],
                               ACT.Copy).then_inc(rounded, 1)

            def read_o(it, h, g):
                a = h % 2
                act.wait_ge(weighted, BL * (HB * it + h) + (BL if g else QB))
                wait(act, o_stored[(G * h + g) % OS], 16 * (G * HB // OS * it + (G * h + g) // OS))
                act.activation(o_both[:, (G * h + g) % OS], p_o[64 * a:64 * a + 64, :], ACT.Copy).then_inc(o_read, 1)

            run({"engine": act, "exp": exp, "round": round_block, "read_o": read_o}, ORDER["scalar"])

        @block.vector
        def _(dve):
            def top_row(it, h, r):
                dve.wait_ge(scored, ROWS * (HB * it + h) + r + 1)
                wait(dve, exped, ROWS * (HB * it + h - 1) + r + 1)
                dve.tensor_reduce(top[:, r:r + 1], p_score[:, r % 2, 0:width_of(r)], AX_X, ALU.max,
                                  negate=True).then_inc(topped, 1)

            def rest(it, h, j):
                g, kb, c0 = block_of(j)
                slot = (BL * h + j) % PT
                dve.wait_ge(rounded, BL * (HB * it + h) + j + 1)
                dve.tensor_tensor(pt_lo[:, slot, c0:W], p_turn[:, (BL * h + j) % TB, c0:W], pt_hi[:, slot, c0:W].bitcast(F32),
                                  ALU.subtract).then_inc(split, 1)

            dve.wait_ge(mask_loaded, 16)
            dve.tensor_copy(mask[:], mask_f[:]).then_inc(masked, 1)
            run({"engine": dve, "top": top_row, "rest": rest}, ORDER["vector"])


def project_out(nc, o_dram, total, ident, wo, v_bias, row, parked, res):
    QUADS = HEADS // 4
    BLK = W // P
    YB = 6
    with ExitStack() as ctx:
        sb, ps, sem = alloc(nc, ctx)
        raw = sb("wo_raw", [P, QUADS, D])
        w_hi = sb("wo_hi", [P, QUADS, D], F32R)
        w_lo = sb("wo_lo", [P, QUADS, D], F32R)
        o = sb("o", [P, 2, QUADS, 2, W])
        o_hi = sb("o_hi", [P, 2, QUADS, W], F32R)
        o_lo = sb("o_lo", [P, 2, QUADS, W], F32R)
        bias = sb("v_bias_sb", [P, QUADS])
        b_row = sb("bo_row", [P, D])
        inv = sb("inv", [P, QUADS, TT, BLK * 4])
        spread = sb("spread", [P, 2, BLK, P])
        p_y = ps("p_y", [P, YB, D])
        p_inv = ps("p_inv", [P, 2, W])
        w_loaded, b_loaded = sem("wo_loaded"), sem("bo_loaded")
        res_loaded = [sem(f"res_loaded{t}") for t in range(TT)]
        o_loaded = [sem(f"o_loaded{i}") for i in range(2)]
        w_rounded, w_split, res_biased = sem("wo_rounded"), sem("wo_split"), sem("res_biased2")
        o_rounded, o_split, y_done, y_added = sem("o_rounded"), sem("o_split"), sem("y_done"), sem("y_added")
        inverted, repeated, inv_turned, divided = sem("inverted"), sem("repeated"), sem("inv_turned"), sem("divided")
        summed = sem("summed")
        block = ctx.enter_context(nc.Block())

        @block.sync
        def _(sp):
            sp.dma_start(bias[:], v_bias).then_inc(b_loaded, 16)
            sp.dma_start(raw[:], wo).then_inc(w_loaded, 16)
            sp.dma_start(b_row[:], row.to_broadcast([P, D])).then_inc(b_loaded, 16)
            old = parked.rearrange("(n p) d -> p n d", p=P)
            for t in range(TT):
                if t >= 2:
                    sp.wait_ge(o_split, t - 1)
                for half in range(2):
                    sp.dma_start(o[:, t % 2, :, half], o_dram[:, half, :, t * W:(t + 1) * W].rearrange("q p t -> p q t"))\
                        .then_inc(o_loaded[t % 2], 16)
                sp.dma_start(res[:, BLK * t:BLK * t + BLK], old[:, BLK * t:BLK * t + BLK]).then_inc(res_loaded[t], 16)

        @block.gpsimd
        def _(pool):
            def add_halves(t):
                pool.wait_ge(o_loaded[t % 2], 32 * (t // 2 + 1))
                for q in range(QUADS):
                    pool.tensor_tensor(o[:, t % 2, q, 0], o[:, t % 2, q, 0], o[:, t % 2, q, 1], ALU.add).then_inc(summed, 1)

            pool.wait_ge(w_loaded, 16)
            pool.tensor_scalar(w_hi[:], raw[:], 1.0, 0.0, ALU.mult, ALU.add).then_inc(w_rounded, 1)
            add_halves(0)
            pool.wait_ge(b_loaded, 32)
            for t in range(TT):
                if t + 1 < TT:
                    add_halves(t + 1)
                pool.wait_ge(res_loaded[t], 16)
                for i in range(BLK * t, BLK * t + BLK):
                    pool.tensor_tensor(res[:, i], res[:, i], b_row[:], ALU.add).then_inc(res_biased, 1)

        @block.scalar
        def _(act):
            def repeat(n):
                if n >= 2:
                    act.wait_ge(inv_turned, n - 1)
                act.activation(spread[:, n % 2].rearrange("p i (h e) -> p (i h) e", h=4),
                               inv[:, n % QUADS, n // QUADS].unsqueeze(2).to_broadcast([P, BLK * 4, E]),
                               ACT.Copy).then_inc(repeated, 1)

            act.wait_ge(inverted, 1)
            repeat(0)
            repeat(1)
            act.wait_ge(b_loaded, 32)
            for t in range(TT):
                if t >= 2:
                    act.wait_ge(y_done, BLK * (t - 1))
                for q in range(QUADS):
                    n = QUADS * t + q
                    if n + 2 < QUADS * TT:
                        repeat(n + 2)
                    act.wait_ge(divided, n + 1)
                    act.activation(o_hi[:, t % 2, q], o[:, t % 2, q, 0], ACT.Identity, bias=bias[:, q:q + 1]).then_inc(o_rounded, 1)

        @block.vector
        def _(dve):
            def add(t):
                for i in range(BLK * t, BLK * t + BLK):
                    dve.wait_ge(y_done, i + 1)
                    dve.wait_ge(res_biased, i + 1)
                    dve.tensor_tensor(res[:, i], res[:, i], p_y[:, i % YB], ALU.add).then_inc(y_added, 1)

            dve.reciprocal(inv[:].rearrange("p q t i -> p (q t i)"), total[:, :]).then_inc(inverted, 1)
            dve.wait_ge(w_rounded, 1)
            dve.tensor_tensor(w_lo[:], raw[:], w_hi[:].bitcast(F32), ALU.subtract).then_inc(w_split, 1)
            for t in range(TT):
                for q in range(QUADS):
                    dve.wait_ge(inv_turned, QUADS * t + q + 1)
                    dve.wait_ge(summed, QUADS * t + q + 1)
                    dve.tensor_tensor(o[:, t % 2, q, 0], o[:, t % 2, q, 0], p_inv[:, q % 2], ALU.mult).then_inc(divided, 1)
                for q in range(QUADS):
                    dve.wait_ge(o_rounded, QUADS * t + q + 1)
                    ins = dve.scalar_tensor_tensor(o_lo[:, t % 2, q], o[:, t % 2, q, 0], bias[:, q:q + 1],
                                                   o_hi[:, t % 2, q].bitcast(F32), ALU.add, ALU.subtract)
                ins.then_inc(o_split, 1)
                if t:
                    add(t - 1)
            add(TT - 1)

        @block.tensor
        def _(pe):
            def turn_inverses(t):
                for n in range(QUADS * t, QUADS * t + QUADS):
                    pe.wait_ge(repeated, n + 1)
                    if n >= 2:
                        pe.wait_ge(divided, n - 1)
                    for i in range(BLK):
                        mm = pe.matmul(p_inv[:, n % 2, i * P:(i + 1) * P], spread[:, n % 2, i], ident[:, :],
                                       start=True, stop=True)
                    mm.then_inc(inv_turned, 1)

            turn_inverses(0)
            pe.wait_ge(w_split, 1)
            for t in range(TT):
                if t + 1 < TT:
                    turn_inverses(t + 1)
                pe.wait_ge(o_split, t + 1)
                for i in range(BLK * t, BLK * t + BLK):
                    if i >= YB:
                        pe.wait_ge(y_added, i - YB + 1)
                    rows = slice(i % BLK * P, (i % BLK + 1) * P)
                    for q in range(QUADS):
                        pe.matmul(p_y[:, i % YB], o_hi[:, t % 2, q, rows], w_hi[:, q], start=(q == 0), stop=False)
                        pe.matmul(p_y[:, i % YB], o_hi[:, t % 2, q, rows], w_lo[:, q], start=False, stop=False)
                        mm = pe.matmul(p_y[:, i % YB], o_lo[:, t % 2, q, rows], w_hi[:, q], start=False,
                                       stop=(q == QUADS - 1))
                    mm.then_inc(y_done, 1)


def store(nc, res, out):
    with ExitStack() as ctx:
        _, _, sem = alloc(nc, ctx)
        out_stored = sem("out_stored")
        block = ctx.enter_context(nc.Block())

        @block.sync
        def _(sp):
            sp.dma_start(out.rearrange("(n p) d -> p n d", p=P), res[:]).then_inc(out_stored, 16)
            sp.wait_ge(out_stored, 16)


def two_layers(nc, t, out):
    w2f = nc.dram_tensor("w2_rotated", [HID // P, P, D], F32, kind="Internal").ap()
    parked = nc.dram_tensor("res_parked", [T, D], F32, kind="Internal").ap()
    qk_dram = nc.dram_tensor("qk_parked", [HEADS // 2 * B, 2, P, S], F32, kind="Internal").ap()
    v_dram = nc.dram_tensor("v_parked", [HEADS // 4 * B, P, 8 * S // P * E], F32, kind="Internal").ap()
    o_dram = nc.dram_tensor("o_parked", [HEADS // 4, 2, P, T], F32, kind="Internal").ap()
    with ExitStack() as ctx:
        sb, _, _ = alloc(nc, ctx)
        ident = sb("ident", [P, P])
        x_hi = sb("x_hi", [P, KD, T], F32R)
        x_lo = sb("x_lo", [P, KD, T], F32R)
        with ExitStack() as layer0:
            res = alloc(nc, layer0)[0]("res0", [P, NT, D])
            with ExitStack() as front:
                n1 = alloc(nc, front)[0]("n1", [P, NT, D])
                phase(nc, prepare, t["x"], t["w2t"], t["signs"], t["eye"], w2f, ident, res, n1, x_hi, x_lo)
                phase(nc, state_space_branch, t["cols"], t["rank"], t["rows"], ident, res, n1)
            phase(nc, feed_forward, "ff0", t["wgu0"], w2f.rearrange("(g c) p d -> g c p d", c=NC), x_hi, x_lo, res, False)
            phase(nc, renorm, res, parked, ident, x_hi, x_lo)
        phase(nc, project_qkv, t["wqk"], t["wv"], t["qk_bias"], t["qk_scale"], x_hi, x_lo, qk_dram, v_dram)
        total = sb("total", [P, HEADS * NT])
        phase(nc, attention, t["masks"], ident, qk_dram, v_dram, o_dram, total)
        with ExitStack() as layer1:
            res = alloc(nc, layer1)[0]("res1", [P, NT, D])
            phase(nc, project_out, o_dram, total, ident, t["wo"], t["v_bias"], t["bo"], parked, res)
            phase(nc, feed_forward, "ff1", t["wgu1"], t["wd1"], x_hi, x_lo, res, True)
            store(nc, res, out)


def lay_out(inputs):
    import numpy as np

    a = {n: np.asarray(v) for n, v in inputs.items()}
    l0 = {n[8:]: v for n, v in a.items() if n.startswith("L0_attn_")}
    f32 = np.float32

    def by_chunk(w):
        return w.reshape(KD, P, -1).transpose(1, 0, 2).reshape(P, -1)

    def in_order(w):
        return w.reshape(KD, P, NG, NC, P).transpose(2, 3, 1, 0, 4)

    def by_four(w):
        return w.reshape(KD, P, NG, P, NC).transpose(2, 4, 1, 0, 3)

    hadamard = np.ones((1, 1), f32)
    while hadamard.shape[0] < P:
        hadamard = np.block([[hadamard, hadamard], [hadamard, -hadamard]])
    w_qkv, b_qkv = a["L1_attn_W_qkv"], a["L1_attn_b_qkv"]
    quads = HEADS // 4
    qk = w_qkv.T.reshape(KD, P, 3, quads, 2, 2 * E)[:, :, :2].transpose(3, 4, 1, 0, 2, 5)
    v = w_qkv.T.reshape(KD, P, 3, quads, P)[:, :, 2].transpose(2, 1, 0, 3)
    qk_scale = np.ones((P, 1), f32)
    qk_scale[:2 * E] = f32(1) / np.sqrt(f32(E))
    masks = np.zeros((P, 2, P), f32)
    masks[:, 0] = np.where(np.arange(P) > np.arange(P)[:, None], f32(-3e38), f32(0))
    masks[:, 1] = np.eye(P)
    arrays = {
        "x": a["L0_attn_x"].reshape(T, D),
        "w2t": a["L0_ffn_W2"].T,
        "signs": np.stack([hadamard, -hadamard], 1),
        "eye": np.eye(P, dtype=f32),
        "cols": np.concatenate([by_chunk(l0[n]) for n in ("ln_gamma", "ln_beta", "W_in", "W_down")], 1),
        "rank": np.concatenate([l0[n][:, None] for n in ("b_in", "decay_logit", "b_down")] + [l0["W_out"], l0["W_up"]], 1),
        "rows": np.concatenate([l0[n] for n in ("ln_gamma", "ln_beta", "D_skip", "b_out", "b_up")])[None],
        "wgu0": np.stack([in_order(a["L0_ffn_W1"].T), in_order(a["L0_ffn_W3"].T)], 3),
        "wqk": qk.reshape(quads, 2, P, KD, P),
        "wv": v,
        "qk_bias": b_qkv.reshape(3, quads, 2, 2 * E)[:2].transpose(0, 3, 1, 2).reshape(P, 2 * quads),
        "qk_scale": qk_scale,
        "masks": masks,
        "wo": a["L1_attn_W_out"].T.reshape(quads, P, D).transpose(1, 0, 2),
        "v_bias": b_qkv[2 * D:].reshape(quads, P).T,
        "bo": a["L1_attn_b_out"][None],
        "wgu1": np.stack([by_four(a["L1_ffn_w_gate"]), by_four(a["L1_ffn_w_up"])], 3),
        "wd1": a["L1_ffn_w_down"].reshape(NG, P, NC, D).transpose(0, 2, 1, 3),
    }
    return {n: np.ascontiguousarray(v) for n, v in arrays.items()}


def kernel(**inputs):
    import concourse.bacc as bacc
    from concourse.bass_utils import run_bass_kernel_spmd

    nc = bacc.Bacc("TRN2", target_bir_lowering=False, num_devices=1)
    arrays = {f"in_{n}": v for n, v in lay_out(inputs).items()}
    aps = {n[3:]: nc.dram_tensor(n, v.shape, mybir.dt.from_np(v.dtype), kind="ExternalInput").ap() for n, v in arrays.items()}
    out = nc.dram_tensor("out_0", (T, D), F32, kind="ExternalOutput").ap()
    two_layers(nc, aps, out)
    got = run_bass_kernel_spmd(nc, [arrays], core_ids=[0])
    return got.results[0]["out_0"].reshape(B, S, D)
```

```python
from contextlib import ExitStack

import concourse.bass as bass
from concourse import mybir

F32 = mybir.dt.float32
F32R = mybir.dt.float32r
BF16 = mybir.dt.bfloat16
ALU = mybir.AluOpType
ACT = mybir.ActivationFunctionType
AX_X = mybir.AxisListType.X

P = 128
B, S, D = 2, 1024, 512
T = B * S
NT = T // P
KD = D // P
HID = 2048
NC = 4
NG = HID // (NC * P)
W = 512
TT = T // W
HEADS, E = 16, 32
EPS = 1e-5


def alloc(nc, ctx):
    sems = []

    def sb(name, shape, dt=F32):
        return ctx.enter_context(nc.sbuf_tensor(name, shape, dt))

    def ps(name, shape, dt=F32):
        return ctx.enter_context(nc.psum_tensor(name, shape, dt))

    def sem(name):
        sems.append(nc.alloc_semaphore(name))
        return sems[-1]

    ctx.callback(lambda: sems and nc.clear_and_free_semaphores(sems))
    return sb, ps, sem


def phase(nc, program, *args):
    program(nc, *args)
    nc.all_engine_barrier()


def feed_forward(nc, tag, wgu, wd, x_hi, x_lo, res, sparse, out, then_norm):
    UC = NC * TT
    with ExitStack() as ctx:
        sb, ps, sem = alloc(nc, ctx)
        raw_gu = sb(f"{tag}_raw_gu", [P, 2, 2, KD, P])
        raw_d = sb(f"{tag}_raw_d", [P, 2, D])
        gu_hi = sb(f"{tag}_gu_hi", [P, NC, 2, KD, P], F32R)
        gu_lo = sb(f"{tag}_gu_lo", [P, NC, 2, KD, P], F32R)
        d_hi = sb(f"{tag}_d_hi", [P, NC, D], F32R)
        d_lo = sb(f"{tag}_d_lo", [P, NC, D], F32R)
        hid = sb(f"{tag}_hid", [P, 2, NC, W])
        h_hi = sb(f"{tag}_h_hi", [P, NC, W], F32R)
        h_lo = sb(f"{tag}_h_lo", [P, NC, W], F32R)
        if sparse:
            mag = sb(f"{tag}_mag", [P, 2, W])
            top = sb(f"{tag}_top", [P, 2, W])
            low = sb(f"{tag}_low", [P, 2, W])
            first = sb(f"{tag}_first", [P, 2, W], BF16)
            both = sb(f"{tag}_both", [P, 2, W], BF16)
            vote = sb(f"{tag}_vote", [P, 2, W], BF16)
        one = sb(f"{tag}_one", [P, 1])
        p_gate = ps(f"{tag}_p_gate", [P, 2, W])
        p_up = ps(f"{tag}_p_up", [P, 2, W])
        p_out = ps(f"{tag}_p_out", [P, W // P, D])

        gu_loaded = [sem(f"{tag}_gu_loaded{i}") for i in range(2)]
        d_loaded = [sem(f"{tag}_d_loaded{i}") for i in range(2)]
        gu_rounded, gu_split = sem(f"{tag}_gu_rounded"), sem(f"{tag}_gu_split")
        d_rounded, d_split = sem(f"{tag}_d_rounded"), sem(f"{tag}_d_split")
        gate_done, up_done = sem(f"{tag}_gate_done"), sem(f"{tag}_up_done")
        silu_done, hid_done = sem(f"{tag}_silu_done"), sem(f"{tag}_hid_done")
        mag_done, choice = sem(f"{tag}_mag_done"), sem(f"{tag}_choice")
        hi_done, lo_done = sem(f"{tag}_hi_done"), sem(f"{tag}_lo_done")
        out_done, added = sem(f"{tag}_out_done"), sem(f"{tag}_added")
        one_set = sem(f"{tag}_one_set")
        stored = [sem(f"{tag}_stored{t}") for t in range(TT)]
        if then_norm:
            vec_stats, act_sd, vec_norm, _ = norm_steps(nc, ctx, "n4", res, res)
        CH = 17

        block = ctx.enter_context(nc.Block())

        @block.sync
        def _(sp):
            def load_gu(g, c, first_group):
                if not (first_group and c < 2):
                    sp.wait_ge(gu_split, NC * g + c - 1)
                sp.dma_start(raw_gu[:, c % 2], wgu[g, c]).then_inc(gu_loaded[c % 2], 16)

            def load_d(g, c, first_group):
                if not (first_group and c < 2):
                    sp.wait_ge(d_split, NC * g + c - 1)
                sp.dma_start(raw_d[:, c % 2], wd[g, c]).then_inc(d_loaded[c % 2], 16)

            for c in range(NC):
                load_gu(0, c, True)
                load_d(0, c, True)
            with sp.Fori(1, NG) as g:
                for c in range(NC):
                    load_gu(g, c, False)
                for c in range(NC):
                    load_d(g, c, False)
            rows = out.rearrange("(n p) d -> p n d", p=P)
            for t in range(TT):
                for j in range(0, W // P, 2):
                    i = t * (W // P) + j
                    sp.wait_ge(added, (W // P) * (TT * NG - TT + t) + j + 2)
                    sp.dma_start(rows[:, i:i + 2], res[:, i:i + 2]).then_inc(stored[t], 16)
            for t in range(TT):
                sp.wait_ge(stored[t], 32)

        @block.gpsimd
        def _(pool):
            def group(g, first_group=False):
                for c in range(NC):
                    n = NC * g + c
                    if first_group:
                        down_piece(g, c, n)
                        continue
                    pool.wait_ge(gu_loaded[c % 2], 16 * (2 * g + c // 2 + 1))
                    pool.wait_ge(up_done, UC * g - NC + c + 1)
                    pool.tensor_tensor(gu_hi[:, c].rearrange("p j k m -> p (j k m)"),
                                       raw_gu[:, c % 2].rearrange("p j k m -> p (j k m)"),
                                       one[:, :].to_broadcast([P, 2 * KD * P]), ALU.mult).then_inc(gu_rounded, 1)
                    pool.wait_ge(gu_rounded, n + 1)
                    pool.tensor_tensor(gu_lo[:, c], raw_gu[:, c % 2], gu_hi[:, c].bitcast(F32),
                                       ALU.subtract).then_inc(gu_split, 1)
                if not first_group:
                    pool.wait_ge(out_done, TT * g)
                    for c in range(NC):
                        down_piece(g, c, NC * g + c)

            def down_piece(g, c, n):
                pool.wait_ge(d_loaded[c % 2], 16 * (2 * g + c // 2 + 1))
                pool.tensor_tensor(d_hi[:, c], raw_d[:, c % 2], one[:, :].to_broadcast([P, D]),
                                   ALU.mult).then_inc(d_rounded, 1)
                pool.wait_ge(d_rounded, n + 1)
                pool.tensor_tensor(d_lo[:, c], raw_d[:, c % 2], d_hi[:, c].bitcast(F32),
                                   ALU.subtract).then_inc(d_split, 1)

            pool.memset(one[:], 1.0).then_inc(one_set, 1)
            pool.wait_ge(one_set, 1)
            group(0, True)
            with pool.Fori(1, NG) as g:
                group(g)

        @block.tensor
        def _(pe):
            def hidden(g, t, first_group):
                for c in range(NC):
                    n = UC * g + NC * t + c
                    if t == 0:
                        pe.wait_ge(gu_split, NC * g + c + 1)
                    if not (first_group and t == 0 and c < 2):
                        pe.wait_ge(hid_done, n - 1)
                    for j, (acc, done) in enumerate(((p_gate, gate_done), (p_up, up_done))):
                        for k in range(KD):
                            xs = slice(t * W, (t + 1) * W)
                            pe.matmul(acc[:, c % 2], gu_hi[:, c, j, k], x_hi[:, k, xs], start=(k == 0), stop=False)
                            pe.matmul(acc[:, c % 2], gu_hi[:, c, j, k], x_lo[:, k, xs], start=False, stop=False)
                            mm = pe.matmul(acc[:, c % 2], gu_lo[:, c, j, k], x_hi[:, k, xs], start=False,
                                           stop=(k == KD - 1))
                        mm.then_inc(done, 1)

            def output(u, g, first_unit):
                pe.wait_ge(d_split, NC * g + NC)
                if not first_unit:
                    pe.wait_ge(added, (W // P) * u)
                for c in range(NC):
                    pe.wait_ge(lo_done, NC * u + c + 1)
                    for j in range(W // P):
                        rows = slice(j * P, (j + 1) * P)
                        pe.matmul(p_out[:, j], h_hi[:, c, rows], d_hi[:, c], start=(c == 0), stop=False)
                        pe.matmul(p_out[:, j], h_hi[:, c, rows], d_lo[:, c], start=False, stop=False)
                        mm = pe.matmul(p_out[:, j], h_lo[:, c, rows], d_hi[:, c], start=False, stop=(c == NC - 1))
                mm.then_inc(out_done, 1)

            def group(g, first_group=False):
                for t in range(TT):
                    hidden(g, t, first_group)
                    if not (first_group and t == 0):
                        gp = g if t else g - 1
                        output(TT * g + t - 1, gp, first_group and t == 1)

            group(0, True)
            with pe.Fori(1, NG) as g:
                group(g)
            output(TT * NG - 1, NG - 1, False)

        @block.scalar
        def _(act):
            def unit(g, t, first_group):
                u = TT * g + t
                s = t % 2
                for c in range(NC):
                    n = NC * u + c
                    act.wait_ge(gate_done, n + 1)
                    if not (first_group and t < 2):
                        act.wait_ge(lo_done, n - 2 * NC + 1)
                    act.activation(hid[:, s, c], p_gate[:, c % 2], ACT.Silu).then_inc(silu_done, 1)
                    if sparse:
                        act.wait_ge(hid_done, n + 1)
                        if c >= 2:
                            act.wait_ge(choice, CH * u + 3)
                        elif not (first_group and t == 0):
                            act.wait_ge(choice, CH * (u - 1) + 6)
                        act.activation(mag[:, c % 2], hid[:, s, c], ACT.Abs).then_inc(mag_done, 1)
                for c in range(NC):
                    n = NC * u + c
                    if sparse:
                        act.wait_ge(choice, CH * u + CH - NC + c + 1)
                    else:
                        act.wait_ge(hid_done, n + 1)
                    if c == 0 and not (first_group and t == 0):
                        act.wait_ge(out_done, u)
                    act.activation(h_hi[:, c], hid[:, s, c], ACT.Copy).then_inc(hi_done, 1)

            def group(g, first_group=False):
                for t in range(TT):
                    unit(g, t, first_group)

            def last_group(g):
                for t in range(TT):
                    unit(g, t, False)
                    if t >= 2:
                        act_sd(act, t - 2)
                act_sd(act, 2)
                act_sd(act, 3)

            for c in range(NC):
                act.wait_ge(gu_loaded[c % 2], 16 * (c // 2 + 1))
                act.activation(gu_hi[:, c], raw_gu[:, c % 2], ACT.Copy).then_inc(gu_rounded, 1)
            group(0, True)
            with act.Fori(1, NG - 1 if then_norm else NG) as g:
                group(g)
            if then_norm:
                last_group(NG - 1)

        @block.vector
        def _(dve):
            def unit(g, t, first_group):
                u = TT * g + t
                s = t % 2
                ch = CH * u

                def compare(pair):
                    a, b = mag[:, 0], mag[:, 1]
                    dve.wait_ge(mag_done, NC * u + 2 * pair + 2)
                    if pair == 0 and not (first_group and t == 0):
                        dve.wait_ge(choice, ch)
                    dve.tensor_tensor(top[:, pair], a, b, ALU.max).then_inc(choice, 1)
                    dve.tensor_tensor(low[:, pair], a, b, ALU.min).then_inc(choice, 1)
                    dve.tensor_tensor(first[:, pair], a, b, ALU.is_ge).then_inc(choice, 1)

                def choose():
                    dve.wait_ge(choice, ch + 6)
                    dve.tensor_tensor(both[:, 0], low[:, 0], top[:, 1], ALU.is_ge).then_inc(choice, 1)
                    dve.tensor_tensor(both[:, 1], low[:, 1], top[:, 0], ALU.is_gt).then_inc(choice, 1)
                    dve.wait_ge(choice, ch + 8)
                    lead = both[:, 0]
                    dve.tensor_tensor(lead, both[:, 0], both[:, 1], ALU.subtract).then_inc(choice, 1)
                    dve.wait_ge(choice, ch + 9)
                    dve.tensor_tensor(vote[:, 0], first[:, 0], lead, ALU.add).then_inc(choice, 1)
                    dve.tensor_tensor(vote[:, 1], first[:, 1], lead, ALU.subtract).then_inc(choice, 1)
                    dve.wait_ge(choice, ch + 11)
                    dve.tensor_tensor(first[:, 0], first[:, 0], lead, ALU.subtract).then_inc(choice, 1)
                    dve.tensor_tensor(first[:, 1], first[:, 1], lead, ALU.add).then_inc(choice, 1)
                    dve.wait_ge(choice, ch + 13)
                    for c, (votes, op, bound) in enumerate(((vote[:, 0], ALU.is_ge, 1.0), (first[:, 0], ALU.is_le, 0.0),
                                                            (vote[:, 1], ALU.is_ge, 1.0), (first[:, 1], ALU.is_le, 0.0))):
                        dve.scalar_tensor_tensor(hid[:, s, c], votes, bound, hid[:, s, c], op,
                                                 ALU.mult).then_inc(choice, 1)

                for c in range(NC):
                    n = NC * u + c
                    dve.wait_ge(silu_done, n + 1)
                    dve.wait_ge(up_done, n + 1)
                    dve.tensor_tensor(hid[:, s, c], hid[:, s, c], p_up[:, c % 2], ALU.mult).then_inc(hid_done, 1)
                    if sparse and c % 2:
                        compare(c // 2)
                if sparse:
                    choose()
                for c in range(NC):
                    dve.wait_ge(hi_done, NC * u + c + 1)
                    dve.tensor_tensor(h_lo[:, c], hid[:, s, c], h_hi[:, c].bitcast(F32),
                                      ALU.subtract).then_inc(lo_done, 1)

            def add_output(u, t):
                dve.wait_ge(out_done, u + 1)
                for j in range(W // P):
                    r = res[:, t * (W // P) + j]
                    dve.tensor_tensor(r, r, p_out[:, j], ALU.add).then_inc(added, 1)

            def group(g, first_group=False):
                for t in range(TT):
                    unit(g, t, first_group)
                    if not (first_group and t == 0):
                        add_output(TT * g + t - 1, (t - 1) % TT)

            def normed(t):
                dve.wait_ge(stored[t], 32)
                vec_norm(dve, t)

            def last_group(g):
                for t in range(TT):
                    unit(g, t, False)
                    add_output(TT * g + t - 1, (t - 1) % TT)
                    if t >= 1:
                        dve.wait_ge(added, (W // P) * (TT * g + t))
                        vec_stats(dve, t - 1)
                    if t >= 3:
                        normed(t - 3)
                normed(1)
                add_output(TT * g + TT - 1, TT - 1)
                dve.wait_ge(added, (W // P) * TT * (g + 1))
                vec_stats(dve, 3)
                normed(2)
                normed(3)

            for c in range(NC):
                dve.wait_ge(gu_rounded, c + 1)
                dve.tensor_tensor(gu_lo[:, c], raw_gu[:, c % 2], gu_hi[:, c].bitcast(F32), ALU.subtract).then_inc(gu_split, 1)
            group(0, True)
            with dve.Fori(1, NG - 1 if then_norm else NG) as g:
                group(g)
            if then_norm:
                last_group(NG - 1)
            else:
                add_output(TT * NG - 1, TT - 1)


def norm_steps(nc, ctx, tag, src, dst, slots=NT):
    sb, _, sem = alloc(nc, ctx)
    Q = NT // 4
    stats = sb(f"{tag}_stats", [P, NT, 6])
    mv = sb(f"{tag}_mv", [P, NT, 2])
    var = sb(f"{tag}_var", [P, NT])
    sd = sb(f"{tag}_sd", [P, NT])
    rstd = sb(f"{tag}_rstd", [P, NT])
    t1 = sb(f"{tag}_t1", [P, NT])
    stat, step, sd_done = sem(f"{tag}_stat"), sem(f"{tag}_step"), sem(f"{tag}_sd_done")
    normed, var_done = sem(f"{tag}_normed"), sem(f"{tag}_var_done")
    NS = 5

    def vec_stats(dve, q):
        for i in range(Q * q, Q * q + Q):
            dve.bn_stats(stats[:, i], src[:, i]).then_inc(stat, 1)
        for i in range(Q * q, Q * q + Q):
            dve.wait_ge(stat, 2 * Q * q + i - Q * q + 1)
            dve.bn_aggr(mv[:, i], stats[:, i]).then_inc(stat, 1)
        dve.wait_ge(stat, 2 * Q * (q + 1))
        a = slice(Q * q, Q * q + Q)
        dve.tensor_scalar(var[:, a], mv[:, a, 1], EPS, None, ALU.add).then_inc(var_done, 1)

    def act_sd(act, q):
        a = slice(Q * q, Q * q + Q)
        act.wait_ge(var_done, q + 1)
        act.activation(sd[:, a], var[:, a], ACT.Sqrt).then_inc(sd_done, 1)

    def vec_norm(dve, q):
        a = slice(Q * q, Q * q + Q)
        s = NS * q
        dve.wait_ge(sd_done, q + 1)
        dve.reciprocal(rstd[:, a], sd[:, a]).then_inc(step, 1)
        dve.wait_ge(step, s + 1)
        dve.tensor_tensor(t1[:, a], rstd[:, a], rstd[:, a], ALU.mult).then_inc(step, 1)
        dve.wait_ge(step, s + 2)
        dve.tensor_tensor(t1[:, a], t1[:, a], var[:, a], ALU.mult).then_inc(step, 1)
        dve.wait_ge(step, s + 3)
        dve.tensor_scalar(t1[:, a], t1[:, a], -0.5, 1.5, ALU.mult, ALU.add).then_inc(step, 1)
        dve.wait_ge(step, s + 4)
        dve.tensor_tensor(rstd[:, a], rstd[:, a], t1[:, a], ALU.mult).then_inc(step, 1)
        dve.wait_ge(step, s + 5)
        for i in range(Q * q, Q * q + Q):
            dve.tensor_scalar(dst[:, i % slots], src[:, i], mv[:, i, 0:1], rstd[:, i:i + 1], ALU.subtract,
                              ALU.mult).then_inc(normed, 1)

    return vec_stats, act_sd, vec_norm, normed


def turn_steps(nc, ctx, tag, src, ident, have, banks, slots=NT):
    _, _, sem = alloc(nc, ctx)
    turned, emptied = sem(f"{tag}_turned"), sem(f"{tag}_emptied")
    NB = banks.shape[1]

    def pe_turn(pe, q):
        if have is not None:
            pe.wait_ge(have, (NT // 4) * (q + 1))
        for k in range(KD):
            m = KD * q + k
            if m >= NB:
                pe.wait_ge(emptied, m - NB + 1)
            for j in range(W // P):
                mm = pe.transpose(banks[:, m % NB, j * P:(j + 1) * P],
                                  src[:, ((NT // 4) * q + j) % slots, k * P:(k + 1) * P], ident[:, :])
            mm.then_inc(turned, 1)

    return pe_turn, turned, emptied


def split_turned(nc, ctx, tag, banks, turned, emptied, x_hi, x_lo):
    _, _, sem = alloc(nc, ctx)
    rounded = sem(f"{tag}_rounded")
    NB = banks.shape[1]

    def act_hi(act, q):
        for k in range(KD):
            m = KD * q + k
            act.wait_ge(turned, m + 1)
            act.activation(x_hi[:, k, q * W:(q + 1) * W], banks[:, m % NB], ACT.Copy).then_inc(rounded, 1)

    def vec_lo(dve, q):
        for k in range(KD):
            m = KD * q + k
            dve.wait_ge(rounded, m + 1)
            cols = slice(q * W, (q + 1) * W)
            dve.tensor_tensor(x_lo[:, k, cols], banks[:, m % NB], x_hi[:, k, cols].bitcast(F32),
                              ALU.subtract).then_inc(emptied, 1)

    return act_hi, vec_lo


def prepare(nc, x, w2t, signs, eye, w2f, ident, res, n1, x_hi, x_lo):
    NCH = HID // P
    with ExitStack() as ctx:
        sb, ps, sem = alloc(nc, ctx)
        w2 = sb("w2", [P, NCH, D])
        rot = sb("rot", [P, NCH, D])
        sign = sb("sign", [P, 2, P])
        banks = ps("banks", [P, 4, W])
        p_rot = ps("p_rot", [P, 4, D])
        x_loaded = [sem(f"x_loaded{q}") for q in range(4)]
        w2_loaded = [sem(f"w2_loaded{q}") for q in range(4)]
        sign_loaded, eye_loaded = sem("sign_loaded"), sem("eye_loaded")
        rot_done, rot_copied, flown, w2f_stored = sem("rot_done"), sem("rot_copied"), sem("flown"), sem("w2f_stored")
        flown_first = sem("flown_first")
        vec_stats, act_sd, vec_norm, normed = norm_steps(nc, ctx, "n1", res, n1)
        pe_turn, turned, emptied = turn_steps(nc, ctx, "t1", n1, ident, normed, banks)
        act_hi, vec_lo = split_turned(nc, ctx, "s1", banks, turned, emptied, x_hi, x_lo)
        block = ctx.enter_context(nc.Block())

        @block.sync
        def _(sp):
            xt = x.rearrange("(n p) d -> p n d", p=P)
            w2c = w2t.rearrange("(n p) d -> p n d", p=P)
            sp.dma_start(ident[:], eye).then_inc(eye_loaded, 16)
            sp.dma_start(sign[:], signs).then_inc(sign_loaded, 16)
            for q in range(4):
                sp.dma_start(res[:, 4 * q:4 * q + 4], xt[:, 4 * q:4 * q + 4]).then_inc(x_loaded[q], 16)
                if q:
                    sp.dma_start(w2[:, 4 * q - 4:4 * q], w2c[:, 4 * q - 4:4 * q]).then_inc(w2_loaded[q - 1], 16)
            sp.dma_start(w2[:, 12:16], w2c[:, 12:16]).then_inc(w2_loaded[3], 16)
            out = w2f.rearrange("n p d -> p n d")
            for h in range(2):
                sp.wait_ge(flown, 4 + h + 1)
                sp.dma_start(out[:, 8 * h:8 * h + 8], w2[:, 8 * h:8 * h + 8]).then_inc(w2f_stored, 16)
            sp.wait_ge(w2f_stored, 32)

        @block.tensor
        def _(pe):
            pe.wait_ge(eye_loaded, 16)
            pe.wait_ge(sign_loaded, 16)

            def rotate(q):
                pe.wait_ge(w2_loaded[q], 16)
                for n in range(4 * q, 4 * q + 4):
                    a, s = n // 2 * 2, n % 2
                    if n >= 4:
                        pe.wait_ge(rot_copied, n - 3)
                    pe.matmul(p_rot[:, n % 4], sign[:, 0], w2[:, a], start=True, stop=False)
                    pe.matmul(p_rot[:, n % 4], sign[:, s], w2[:, a + 1], start=False, stop=True).then_inc(rot_done, 1)

            pe_turn(pe, 0)
            for q in range(1, 4):
                pe_turn(pe, q)
                rotate(q - 1)
            rotate(3)

        @block.scalar
        def _(act):
            def copy_rotated(q):
                for n in range(4 * q, 4 * q + 4):
                    act.wait_ge(rot_done, n + 1)
                    act.activation(rot[:, n], p_rot[:, n % 4], ACT.Copy, scale=float(1.0 / HID ** 0.5)).then_inc(rot_copied, 1)

            act_sd(act, 0)
            act_sd(act, 1)
            act_hi(act, 0)
            for q in range(2, 4):
                act_sd(act, q)
                act_hi(act, q - 1)
                copy_rotated(q - 2)
            act_hi(act, 3)
            copy_rotated(2)
            copy_rotated(3)

        @block.vector
        def _(dve):
            dve.wait_ge(x_loaded[0], 16)
            vec_stats(dve, 0)
            for q in range(4):
                if q < 3:
                    dve.wait_ge(x_loaded[q + 1], 16)
                    vec_stats(dve, q + 1)
                vec_norm(dve, q)
                if q:
                    vec_lo(dve, q - 1)
            vec_lo(dve, 3)
            for h in range(2):
                dve.wait_ge(flown_first, 4 * (h + 1))
                a, b = w2[:, 8 * h:8 * h + 8], rot[:, 8 * h:8 * h + 8]
                dve.tensor_tensor(b[:, 0:4], a[:, 0:4], a[:, 4:8], ALU.add).then_inc(flown, 1)
                dve.tensor_tensor(b[:, 4:8], a[:, 0:4], a[:, 4:8], ALU.subtract).then_inc(flown, 1)
            dve.wait_ge(flown, 4)
            dve.tensor_tensor(w2[:, 0:8], rot[:, 0:8], rot[:, 8:16], ALU.add).then_inc(flown, 1)
            dve.tensor_tensor(w2[:, 8:16], rot[:, 0:8], rot[:, 8:16], ALU.subtract).then_inc(flown, 1)

        @block.gpsimd
        def _(pool):
            for q in range(4):
                pool.wait_ge(rot_copied, 4 * (q + 1))
                a, b = rot[:, 4 * q:4 * q + 4], w2[:, 4 * q:4 * q + 4]
                pool.tensor_tensor(b[:, 0:2], a[:, 0:2], a[:, 2:4], ALU.add).then_inc(flown_first, 1)
                pool.tensor_tensor(b[:, 2:4], a[:, 0:2], a[:, 2:4], ALU.subtract).then_inc(flown_first, 1)


def state_space_branch(nc, cols, rank, ident, res, n1):
    R = rank.shape[0] - 1
    Q = NT // 4
    ZS = 2 * Q
    with ExitStack() as ctx:
        sb, ps, sem = alloc(nc, ctx)
        z = sb("z", [P, ZS, D])
        zT = sb("zT", [P, 4, KD, W])
        col = sb("col", [P, cols.shape[1]])
        diagonal = sb("diagonal", [P, KD, P])
        low = sb("low", [R + 1, T])
        rk = sb("rk", [R + 1, rank.shape[1]])
        decay = sb("decay", [R, 1])
        ones = sb("ones", [R, S])
        gamma, beta, skip = (col[:, KD * i:KD * i + KD] for i in range(3))
        w_in, w_down = (col[:, KD * (3 + R * i):KD * (3 + R * i + R)].rearrange("p (k r) -> p k r", k=KD) for i in range(2))
        b_in, logit, b_down = (rk[0:R, i:i + 1] for i in range(3))
        w_out, w_up = rk[:, 3:3 + D], rk[:, 3 + D:3 + 2 * D]
        banks = ps("ssm_banks", [P, 4, W])
        p_low = ps("p_low", [R, W])
        p_wide = ps("p_wide", [P, 3, D])

        loaded, ones_set, decay_step, diagonal_made = sem("loaded"), sem("ones_set"), sem("decay_step"), sem("diagonal_made")
        low_done, low_copied, scanned = sem("low_done"), sem("low_copied"), sem("scanned")
        wide_done, wide_added, res_x1 = sem("wide_done"), sem("wide_added"), sem("res_x1")
        stats1, sd1, norm1, normed1 = norm_steps(nc, ctx, "n2", n1, z, ZS)
        stats2, sd2, norm2, normed2 = norm_steps(nc, ctx, "n3", n1, z, ZS)
        turn1, turned1, shifted1 = turn_steps(nc, ctx, "t2", z, ident, normed1, banks, ZS)
        turn2, turned2, shifted2 = turn_steps(nc, ctx, "t3", z, ident, normed2, banks, ZS)
        block = ctx.enter_context(nc.Block())

        @block.sync
        def _(sp):
            sp.dma_start(col[:], cols).then_inc(loaded, 16)
            sp.dma_start(rk[:], rank).then_inc(loaded, 16)

        @block.gpsimd
        def _(pool):
            pool.memset(ones[:], 1.0).then_inc(ones_set, 1)
            pool.memset(low[:], 1.0).then_inc(ones_set, 1)
            pool.wait_ge(loaded, 32)
            for k in range(KD):
                pool.tensor_scalar(diagonal[:, k], ident[:, :], skip[:, k:k + 1], None, ALU.mult).then_inc(diagonal_made, 1)
            for i in range(NT):
                pool.wait_ge(wide_added, i + 1)
                pool.tensor_tensor(res[:, i], res[:, i], n1[:, i], ALU.add).then_inc(res_x1, 1)

        @block.tensor
        def _(pe):
            def low_rank(w, shifted, q, n):
                pe.wait_ge(shifted, KD * (q + 1))
                if n:
                    pe.wait_ge(low_copied, n)
                for k in range(KD):
                    mm = pe.matmul(p_low[:, :], w[:, k], zT[:, q, k], start=(k == 0), stop=(k == KD - 1))
                mm.then_inc(low_done, 1)

            def widen_states(q):
                if q % 2 == 0:
                    pe.wait_ge(scanned, q // 2 + 1)
                for i in range(Q * q, Q * q + Q):
                    if i >= 3:
                        pe.wait_ge(wide_added, i - 2)
                    pe.matmul(p_wide[:, i % 3], low[:, i * P:(i + 1) * P], w_out, start=True, stop=False)
                    for k in range(KD):
                        mm = pe.matmul(p_wide[:, i % 3, k * P:(k + 1) * P], zT[:, q, k, (i % Q) * P:(i % Q + 1) * P],
                                       diagonal[:, k], start=False, stop=(k == KD - 1))
                    mm.then_inc(wide_done, 1)

            def widen_up(q):
                pe.wait_ge(low_copied, 4 + q + 1)
                for i in range(Q * q, Q * q + Q):
                    pe.wait_ge(wide_added, NT + i - 2)
                    pe.matmul(p_wide[:, (NT + i) % 3], low[:, i * P:(i + 1) * P], w_up, start=True,
                              stop=True).then_inc(wide_done, 1)

            turn1(pe, 0)
            turn1(pe, 1)
            pe.wait_ge(loaded, 32)
            low_rank(w_in, shifted1, 0, 0)
            turn1(pe, 2)
            low_rank(w_in, shifted1, 1, 1)
            turn1(pe, 3)
            low_rank(w_in, shifted1, 2, 2)
            pe.wait_ge(diagonal_made, KD)
            widen_states(0)
            low_rank(w_in, shifted1, 3, 3)
            widen_states(1)
            pe.wait_ge(shifted1, 4 * KD)
            turn2(pe, 0)
            widen_states(2)
            turn2(pe, 1)
            low_rank(w_down, shifted2, 0, 4)
            widen_states(3)
            turn2(pe, 2)
            low_rank(w_down, shifted2, 1, 5)
            turn2(pe, 3)
            widen_up(0)
            low_rank(w_down, shifted2, 2, 6)
            widen_up(1)
            low_rank(w_down, shifted2, 3, 7)
            widen_up(2)
            widen_up(3)

        @block.scalar
        def _(act):
            def shift(q, turned, shifted, again):
                if again:
                    act.wait_ge(wide_done, Q * (q + 1))
                for k in range(KD):
                    m = KD * q + k
                    act.wait_ge(turned, m + 1)
                    act.activation(zT[:, q, k], banks[:, m % 4], ACT.Identity, bias=beta[:, k:k + 1],
                                   scale=gamma[:, k:k + 1]).then_inc(shifted, 1)

            def low_copy(q, again):
                act.wait_ge(low_done, 4 * again + q + 1)
                if again:
                    act.wait_ge(wide_done, Q * (q + 1))
                act.activation(low[0:R, q * W:(q + 1) * W], p_low[:, :], ACT.Relu if again else ACT.Identity,
                               bias=b_down if again else b_in).then_inc(low_copied, 1)

            act.wait_ge(loaded, 32)
            act.activation(decay[:], logit, ACT.Sigmoid).then_inc(decay_step, 1)
            act.wait_ge(ones_set, 2)
            sd1(act, 0)
            sd1(act, 1)
            shift(0, turned1, shifted1, False)
            sd1(act, 2)
            shift(1, turned1, shifted1, False)
            low_copy(0, False)
            sd1(act, 3)
            shift(2, turned1, shifted1, False)
            low_copy(1, False)
            shift(3, turned1, shifted1, False)
            low_copy(2, False)
            low_copy(3, False)
            sd2(act, 0)
            sd2(act, 1)
            shift(0, turned2, shifted2, True)
            sd2(act, 2)
            shift(1, turned2, shifted2, True)
            low_copy(0, True)
            sd2(act, 3)
            shift(2, turned2, shifted2, True)
            low_copy(1, True)
            shift(3, turned2, shifted2, True)
            low_copy(2, True)
            low_copy(3, True)

        @block.vector
        def _(dve):
            def scan(b):
                dve.wait_ge(low_copied, 2 * (b + 1))
                dve.tensor_tensor_scan(low[0:R, b * S:(b + 1) * S], ones[:], low[0:R, b * S:(b + 1) * S], 0.0, ALU.mult,
                                       ALU.add).then_inc(scanned, 1)

            def add_states(q):
                for i in range(Q * q, Q * q + Q):
                    dve.wait_ge(wide_done, i + 1)
                    dve.tensor_tensor(n1[:, i], n1[:, i], p_wide[:, i % 3], ALU.add).then_inc(wide_added, 1)

            def add_up(q):
                for i in range(Q * q, Q * q + Q):
                    dve.wait_ge(wide_done, NT + i + 1)
                    dve.wait_ge(res_x1, i + 1)
                    dve.tensor_tensor(res[:, i], res[:, i], p_wide[:, (NT + i) % 3], ALU.add).then_inc(wide_added, 1)

            def restats(q):
                dve.wait_ge(wide_added, Q * (q + 1))
                stats2(dve, q)

            def renorm2(q):
                if q < 2:
                    dve.wait_ge(turned1, KD * (q + 3))
                else:
                    dve.wait_ge(turned2, KD * (q - 1))
                norm2(dve, q)

            stats1(dve, 0)
            for q in range(4):
                if q < 3:
                    stats1(dve, q + 1)
                if q >= 2:
                    dve.wait_ge(turned1, KD * (q - 1))
                norm1(dve, q)
                if q == 0:
                    dve.wait_ge(ones_set, 1)
                    dve.wait_ge(decay_step, 1)
                    dve.tensor_scalar(ones[:], ones[:], decay[:], None, ALU.mult).then_inc(decay_step, 1)
            dve.wait_ge(decay_step, 2)
            scan(0)
            add_states(0)
            restats(0)
            add_states(1)
            renorm2(0)
            scan(1)
            restats(1)
            add_states(2)
            renorm2(1)
            restats(2)
            add_states(3)
            renorm2(2)
            restats(3)
            renorm2(3)
            for q in range(4):
                add_up(q)


def turn_and_split(nc, n2, ident, x_hi, x_lo):
    with ExitStack() as ctx:
        _, ps, _ = alloc(nc, ctx)
        banks = ps("banks2", [P, 8, W])
        pe_turn, turned, emptied = turn_steps(nc, ctx, "t4", n2, ident, None, banks)
        act_hi, vec_lo = split_turned(nc, ctx, "s4", banks, turned, emptied, x_hi, x_lo)
        block = ctx.enter_context(nc.Block())

        @block.tensor
        def _(pe):
            for q in range(4):
                pe_turn(pe, q)

        @block.scalar
        def _(act):
            for q in range(4):
                act_hi(act, q)

        @block.vector
        def _(dve):
            for q in range(4):
                vec_lo(dve, q)


STACKS = 8 * 16


def load_stack(sp, stack, qk_dram, it, n, stacked):
    here = qk_dram[4 * it + n]
    for a in range(2):
        for what in range(2):
            r = 2 * E * what + E * a
            src = here[:, r:r + E, :]
            for half in range(2):
                s = src[half].unsqueeze(0).to_broadcast([2, E, S]) if what == 0 else src
                sp.dma_start(stack[64 * half:64 * half + 64, n % 2, a, what].bitcast(F32), s).then_inc(stacked, 16)


def load_values(sp, v, v_dram, quad, b, loaded):
    sp.dma_start(v[:, b].rearrange("p t a h e -> p (t a h e)").bitcast(F32), v_dram[B * quad + b]).then_inc(loaded, 16)


def project_qkv(nc, wqk, wv, qk_bias, qk_scale, masks, x_hi, x_lo, qk_dram, v_dram, stack, v_first, mask):
    QUADS = HEADS // 4
    QK = 2 * B * 2
    BANKS = 4
    with ExitStack() as ctx:
        sb, ps, sem = alloc(nc, ctx)
        raw_w = sb("raw_w", [P, 2, KD, P])
        w_hi = sb("w_hi", [P, 2, KD, P], F32R)
        w_lo = sb("w_lo", [P, 2, KD, P], F32R)
        raw_v = sb("raw_v", [P, KD, D])
        v_hi = sb("v_hi", [P, KD, D], F32R)
        v_lo = sb("v_lo", [P, KD, D], F32R)
        bias = sb("bias", [P, 2 * QUADS])
        pair_bias = sb("pair_bias", [P, 2])
        scale = sb("scale", [P, 1])
        one = sb("one", [P, 1])
        val = sb("val", [P, 2, W])
        qk = sb("qk", [P, 2, 2, S], F32R)
        v = sb("v_out", [P, BANKS, QUADS, 4, 2, E], F32R)
        p_job = ps("p_job", [P, BANKS, W])
        p_v = ps("p_v", [P, BANKS, D])

        consts, one_set, scale_done = sem("consts"), sem("one_set"), sem("scale_done")
        w_loaded = [sem(f"w_loaded{i}") for i in range(2)]
        w_rounded = [sem(f"w_rounded{i}") for i in range(2)]
        w_split = [sem(f"w_split{i}") for i in range(2)]
        w_biased = [sem(f"w_biased{i}") for i in range(2)]
        job_done, job_used = sem("job_done"), sem("job_used")
        qk_rounded, qk_split, v_rounded, v_split = sem("qk_rounded"), sem("qk_split"), sem("v_rounded"), sem("v_split")
        qk_stored = [sem(f"qk_stored{i}") for i in range(2)]
        mask_f = sb("mask_f", [P, 2, P])
        mask_loaded, first_loaded = sem("mask_loaded"), sem("first_loaded")
        v_stored = [sem(f"v_stored{i}") for i in range(BANKS)]
        wv_loaded, wv_rounded, wv_split, v_done = sem("wv_loaded"), sem("wv_rounded"), sem("wv_split"), sem("v_done")
        block = ctx.enter_context(nc.Block())

        @block.sync
        def _(sp):
            def load_w(quad, i, first=False):
                if not first:
                    sp.wait_ge(w_split[i], quad)
                sp.dma_start(raw_w[:, i], wqk[quad, i]).then_inc(w_loaded[i], 16)

            def body(it, last):
                if not last:
                    for i in range(2):
                        load_w(it + 1, i)
                for n in range(4):
                    pair = 2 * (n % 2) + n // 2
                    sp.wait_ge(qk_split, QK * it + 2 * n + 2)
                    sp.dma_start(qk_dram[4 * it + pair].rearrange("h p n -> p h n"), qk[:, n % 2].bitcast(F32))\
                        .then_inc(qk_stored[n % 2], 16)

            load_w(0, 0, True)
            sp.dma_start(bias[:], qk_bias).then_inc(consts, 16)
            sp.dma_start(scale[:], qk_scale).then_inc(consts, 16)
            load_w(0, 1, True)
            for k in range(KD):
                sp.dma_start(raw_v[:, k], wv[:, k]).then_inc(wv_loaded, 16)
            body(0, False)
            for m in range(NT):
                sp.wait_ge(v_split, m + 1)
                b, tb = divmod(m, S // P)
                to = v_dram.rearrange("(q b) p n -> b p q n", b=B)[b, :, :, tb * 8 * E:(tb + 1) * 8 * E]
                sp.dma_start(to, v[:, m % BANKS].rearrange("p q h a e -> p q (h a e)").bitcast(F32))\
                    .then_inc(v_stored[m % BANKS], 16)
                if m in (5, 11):
                    for i in range(2):
                        sp.wait_ge(qk_stored[i], 32)
                    load_stack(sp, stack, qk_dram, 0, m // 6, first_loaded)
            sp.dma_start(mask_f[:], masks).then_inc(mask_loaded, 16)
            for i in range(BANKS):
                sp.wait_ge(v_stored[i], 16 * NT // BANKS)
            for b in range(B):
                load_values(sp, v_first, v_dram, 0, b, first_loaded)
            with sp.Fori(1, QUADS - 1) as it:
                body(it, False)
            body(QUADS - 1, True)
            for i in range(2):
                sp.wait_ge(qk_stored[i], 16 * 2 * QUADS)
            sp.wait_ge(first_loaded, 2 * STACKS + 16 * B)

        @block.gpsimd
        def _(pool):
            def split_w(quad, i, first=False):
                pool.wait_ge(w_loaded[i], 16 * (quad + 1))
                if not first:
                    pool.wait_ge(job_done, QK * (quad - 1) + 4 * i + 4)
                pool.tensor_tensor(w_hi[:, i].rearrange("p k m -> p (k m)"), raw_w[:, i].rearrange("p k m -> p (k m)"),
                                   one[:, :].to_broadcast([P, D]), ALU.mult).then_inc(w_rounded[i], 1)
                pool.wait_ge(w_rounded[i], quad + 1)
                pool.tensor_tensor(w_lo[:, i], raw_w[:, i], w_hi[:, i].bitcast(F32), ALU.subtract).then_inc(w_split[i], 1)

            pool.memset(one[:], 1.0).then_inc(one_set, 1)
            pool.wait_ge(one_set, 1)
            for i in range(2):
                split_w(0, i, True)
            for k in range(KD):
                pool.wait_ge(wv_loaded, 16 * KD)
                pool.tensor_scalar(v_hi[:, k], raw_v[:, k], 1.0, 0.0, ALU.mult, ALU.add).then_inc(wv_rounded, 1)
                pool.wait_ge(wv_rounded, k + 1)
                pool.tensor_tensor(v_lo[:, k], raw_v[:, k], v_hi[:, k].bitcast(F32), ALU.subtract).then_inc(wv_split, 1)
            with pool.Fori(1, QUADS) as quad:
                for i in range(2):
                    split_w(quad, i)

        @block.tensor
        def _(pe):
            def body(it, first):
                for m in range(QK):
                    i = m // 4
                    if m % 4 == 0:
                        pe.wait_ge(w_split[i], it + 1)
                    if not (first and m < BANKS):
                        pe.wait_ge(job_used, QK * it + m + 1 - BANKS)
                    t0 = m % 4 // 2 * S + m % 2 * W
                    for k in range(KD):
                        for y, (w, x) in enumerate(((w_hi, x_hi), (w_hi, x_lo), (w_lo, x_hi))):
                            mm = pe.matmul(p_job[:, m % BANKS], w[:, i, k], x[:, k, t0:t0 + W], start=(k + y == 0),
                                           stop=(k == KD - 1 and y == 2))
                    mm.then_inc(job_done, 1)

            body(0, True)
            pe.wait_ge(wv_split, KD)
            for m in range(NT):
                if m >= BANKS:
                    pe.wait_ge(v_split, m + 1 - BANKS)
                for k in range(KD):
                    for y, (w, x) in enumerate(((v_hi, x_hi), (v_hi, x_lo), (v_lo, x_hi))):
                        mm = pe.matmul(p_v[:, m % BANKS], x[:, k, m * P:(m + 1) * P], w[:, k], start=(k + y == 0),
                                       stop=(k == KD - 1 and y == 2))
                mm.then_inc(v_done, 1)
            with pe.Fori(1, QUADS) as it:
                body(it, False)

        @block.scalar
        def _(act):
            def body(it, first):
                for m in range(QK):
                    i = m // 4
                    act.wait_ge(job_done, QK * it + m + 1)
                    if m % 4 == 0:
                        act.wait_ge(w_biased[i], it + 1)
                    if not (first and m < 2):
                        act.wait_ge(qk_split, QK * it + m - 1)
                    act.activation(val[:, m % 2], p_job[:, m % BANKS], ACT.Identity, bias=pair_bias[:, i:i + 1],
                                   scale=scale[:, 0:1]).then_inc(job_used, 1)

            act.wait_ge(consts, 32)
            body(0, True)
            for m in range(NT):
                act.wait_ge(v_done, m + 1)
                if m >= BANKS:
                    act.wait_ge(v_stored[m % BANKS], 16 * (m // BANKS))
                act.activation(v[:, m % BANKS, :, :, 0, :], p_v[:, m % BANKS].rearrange("p (q h e) -> p q h e", q=QUADS, h=4),
                               ACT.Copy).then_inc(v_rounded, 1)
            with act.Fori(1, QUADS) as it:
                body(it, False)

        @block.vector
        def _(dve):
            def body(it, first):
                for m in range(QK):
                    if m in (0, 4):
                        i = m // 4
                        if not first:
                            dve.wait_ge(job_used, QK * (it - 1) + m + 4)
                        dve.tensor_copy(pair_bias[:, i:i + 1], bias[:, bass.ds(2 * it + i, 1)]).then_inc(w_biased[i], 1)
                    part = m % 2
                    dve.wait_ge(job_used, QK * it + m + 1)
                    if part == 0 and not (first and m < 4):
                        dve.wait_ge(qk_stored[m // 2 % 2], 16 * (2 * it + m // 4))
                    hi, lo = (qk[:, m // 2 % 2, half, part * W:(part + 1) * W] for half in range(2))
                    dve.tensor_copy(hi, val[:, m % 2]).then_inc(qk_rounded, 1)
                    dve.wait_ge(qk_rounded, QK * it + m + 1)
                    dve.tensor_tensor(lo, val[:, m % 2], hi.bitcast(F32), ALU.subtract).then_inc(qk_split, 1)

            dve.wait_ge(consts, 32)
            dve.tensor_scalar(bias[:], bias[:], scale[:, 0:1], None, ALU.mult).then_inc(scale_done, 1)
            dve.wait_ge(scale_done, 1)
            body(0, True)
            for m in range(NT):
                dve.wait_ge(v_rounded, m + 1)
                dve.tensor_tensor(v[:, m % BANKS, :, :, 1, :], p_v[:, m % BANKS].rearrange("p (q h e) -> p q h e", q=QUADS, h=4),
                                  v[:, m % BANKS, :, :, 0, :].bitcast(F32), ALU.subtract).then_inc(v_split, 1)
            dve.wait_ge(mask_loaded, 16)
            dve.tensor_copy(mask[:], mask_f[:])
            with dve.Fori(1, QUADS) as it:
                body(it, False)


def attention(nc, mask, stack, v, ident, qk_dram, v_dram, o_dram, total):
    G = 2
    QB = 4
    QUADS = HEADS // 4
    HB = B * 4
    ROWS = QB * G
    BL = 12
    TB = 3
    PT = 6
    OS = 4
    AHEAD, BEHIND = 2, 1
    ORDER = {
        "tensor": [("weigh", 10, -1), ("weigh", 11, -1), ("turn", 3, 0), ("score", 1, 1), ("turn", 4, 0),
                   ("score", 2, 1), ("turn", 5, 0), ("weigh", 0, 0), ("turn", 6, 0), ("weigh", 1, 0),
                   ("score", 3, 1), ("turn", 7, 0), ("turn", 8, 0), ("score", 4, 1), ("weigh", 2, 0),
                   ("weigh", 3, 0), ("turn", 9, 0), ("score", 5, 1), ("turn", 10, 0), ("weigh", 4, 0),
                   ("weigh", 5, 0), ("score", 6, 1), ("turn", 11, 0), ("weigh", 6, 0), ("turn", 0, 1),
                   ("score", 7, 1), ("weigh", 7, 0), ("turn", 1, 1), ("turn", 2, 1), ("weigh", 8, 0),
                   ("score", 0, 2), ("weigh", 9, 0)],
        "scalar": [("round", 2, 0), ("exp", 0, 1), ("round", 3, 0), ("read_o", 1, -1), ("round", 4, 0),
                   ("round", 5, 0), ("exp", 1, 1), ("exp", 2, 1), ("round", 6, 0), ("round", 7, 0),
                   ("exp", 3, 1), ("round", 8, 0), ("read_o", 0, 0), ("exp", 4, 1), ("round", 9, 0),
                   ("exp", 5, 1), ("round", 10, 0), ("round", 11, 0), ("round", 0, 1), ("exp", 6, 1),
                   ("round", 1, 1), ("exp", 7, 1)],
        "vector": [("rest", 1, 0), ("top", 0, 1), ("rest", 2, 0), ("rest", 3, 0), ("top", 1, 1),
                   ("top", 2, 1), ("rest", 4, 0), ("rest", 5, 0), ("top", 3, 1), ("rest", 6, 0),
                   ("rest", 7, 0), ("top", 4, 1), ("rest", 8, 0), ("top", 5, 1), ("rest", 9, 0),
                   ("top", 6, 1), ("rest", 10, 0), ("rest", 11, 0), ("top", 7, 1), ("rest", 0, 1)],
    }

    with ExitStack() as ctx:
        sb, ps, sem = alloc(nc, ctx)
        prob = [sb("prob0", [P, 2, QB, W]), sb("prob1", [P, 2, QB, S])]
        top = sb("row_top", [P, ROWS])
        pt_hi = sb("pt_hi", [P, PT, W], F32R)
        pt_lo = sb("pt_lo", [P, PT, W], F32R)
        o_both = sb("o_both", [2 * E, OS, W])
        p_score = ps("p_score", [P, 2, S])
        p_turn = ps("p_turn", [P, TB, W])
        p_o = ps("p_o", [P, W])

        stacked = [sem(f"stacked{i}") for i in range(2)]
        scored, topped, exped = sem("scored"), sem("topped"), sem("exped")
        turned, rounded, split, weighted = sem("turned"), sem("rounded"), sem("split"), sem("weighted")
        o_read = sem("o_read")
        v_loaded = [sem(f"v_loaded{b}") for b in range(B)]
        o_stored = [sem(f"o_stored{i}") for i in range(OS)]

        def wait(engine, semaphore, count):
            if not isinstance(count, int) or count > 0:
                engine.wait_ge(semaphore, count)

        def width_of(r):
            return (r + 1) * P

        def place_of(h):
            return h // 4, h // 2 % 2, h % 2

        def block_of(j):
            g, kb = (0, j) if j < QB else (1, j - QB)
            return g, kb, max(0, kb - QB * g) * P

        def run(steps, order):
            def heads(it, hs):
                for h in hs:
                    for step, n, ahead in order:
                        head = h + ahead
                        if isinstance(it, int) and not 0 <= HB * it + head < HB * QUADS:
                            continue
                        steps[step](it + head // HB, head % HB, n)

            heads(0, range(-AHEAD, HB))
            with steps["engine"].Fori(1, QUADS - 1) as it:
                heads(it, range(HB))
            heads(QUADS - 1, range(HB + BEHIND))

        block = ctx.enter_context(nc.Block())

        @block.sync
        def _(sp):
            def next_stack(it, n):
                sp.wait_ge(scored, 2 * ROWS * (4 * it + n - 1))
                load_stack(sp, stack, qk_dram, it, n, stacked[n % 2])

            def next_values(quad, b):
                sp.wait_ge(weighted, HB * BL * quad + (b - 1) * (HB * BL // 2))
                load_values(sp, v, v_dram, quad, b, v_loaded[b])

            def store_o(it, h, g):
                b, pr, a = place_of(h)
                sp.wait_ge(o_read, G * (HB * it + h) + g + 1)
                row, t0 = E * (2 * pr + a), b * S + g * W
                sp.dma_start(o_dram[it, :, row:row + E, t0:t0 + W], o_both[:, (G * h + g) % OS])\
                    .then_inc(o_stored[(G * h + g) % OS], 16)

            def body(it, first, last):
                for h in range(HB):
                    for g in range(G):
                        store_o(it, h, g)
                    n = h // 2 + 2
                    if h % 2 == 0 and not (last and n >= 4):
                        next_stack(it + n // 4, n % 4)
                    if h == 0 and not first:
                        next_values(it, 1)
                    if h == 4 and not last:
                        next_values(it + 1, 0)

            body(0, True, False)
            with sp.Fori(1, QUADS - 1) as it:
                body(it, False, False)
            body(QUADS - 1, False, True)
            for i in range(OS):
                sp.wait_ge(o_stored[i], 16 * (G * HEADS * B // OS))

        @block.tensor
        def _(pe):
            def score(it, h, r):
                pair, a = h // 2, h % 2
                if r == 0 and a == 0:
                    wait(pe, stacked[pair % 2], STACKS * (2 * it + pair // 2))
                wait(pe, exped, ROWS * (HB * it + h) + r - 1)
                q = stack[:, pair % 2, a, 0, r * P:(r + 1) * P]
                for c0 in range(0, width_of(r), W):
                    c1 = min(width_of(r), c0 + W)
                    pe.matmul(p_score[:, r % 2, c0:c1], q, stack[:, pair % 2, a, 1, c0:c1], start=True,
                              stop=c1 < width_of(r))
                pe.matmul(p_score[:, r % 2, r * P:(r + 1) * P], mask[:, 1], mask[:, 0], start=False,
                          stop=True).then_inc(scored, 1)

            def turn(it, h, j):
                g, kb, c0 = block_of(j)
                if kb == 0:
                    pe.wait_ge(exped, ROWS * (HB * it + h) + QB * (g + 1))
                wait(pe, split, BL * (HB * it + h) + j - TB + 1)
                for i in range(c0 // P, QB):
                    mm = pe.transpose(p_turn[:, (BL * h + j) % TB, i * P:(i + 1) * P],
                                      prob[g][:, h % 2, i, kb * P:(kb + 1) * P], ident[:, :])
                mm.then_inc(turned, 1)

            def weigh(it, h, j):
                b, pr, a = place_of(h)
                g, kb, c0 = block_of(j)
                if j == 0 and h % 4 == 0:
                    wait(pe, v_loaded[b], 16 * it)
                if kb == 0:
                    wait(pe, o_read, G * (HB * it + h) + g)
                pe.wait_ge(split, BL * (HB * it + h) + j + 1)
                lhs = v[:, b, kb, 2 * pr:2 * pr + 2].rearrange("p a h e -> p (a h e)")
                slot = (BL * h + j) % PT
                pe.matmul(p_o[:, c0:W], lhs, pt_hi[:, slot, c0:W], start=(kb == 0), stop=False)
                pe.matmul(p_o[:, c0:W], lhs, pt_lo[:, slot, c0:W], start=False,
                          stop=(j in (QB - 1, BL - 1))).then_inc(weighted, 1)

            run({"engine": pe, "score": score, "turn": turn, "weigh": weigh}, ORDER["tensor"])

        @block.scalar
        def _(act):
            def exp(it, h, r):
                b, pr, a = place_of(h)
                act.wait_ge(topped, ROWS * (HB * it + h) + r + 1)
                wait(act, turned, BL * (HB * it + h - 2) + (r + 1 if r < QB else QB + r + 1))
                sums = total[:, bass.ds(QB * G * 4 * (B * it + b) + 4 * r + 2 * pr + a, 1)]
                act.activation(prob[r // QB][:, h % 2, r % QB, 0:width_of(r)], p_score[:, r % 2, 0:width_of(r)], ACT.Exp,
                               bias=top[:, r:r + 1], accum_out=sums).then_inc(exped, 1)

            def round_block(it, h, j):
                g, kb, c0 = block_of(j)
                act.wait_ge(turned, BL * (HB * it + h) + j + 1)
                wait(act, weighted, BL * (HB * it + h) + j - PT + 1)
                act.activation(pt_hi[:, (BL * h + j) % PT, c0:W], p_turn[:, (BL * h + j) % TB, c0:W],
                               ACT.Copy).then_inc(rounded, 1)

            def read_o(it, h, g):
                a = h % 2
                act.wait_ge(weighted, BL * (HB * it + h) + (BL if g else QB))
                wait(act, o_stored[(G * h + g) % OS], 16 * (G * HB // OS * it + (G * h + g) // OS))
                act.activation(o_both[:, (G * h + g) % OS], p_o[64 * a:64 * a + 64, :], ACT.Copy).then_inc(o_read, 1)

            run({"engine": act, "exp": exp, "round": round_block, "read_o": read_o}, ORDER["scalar"])

        @block.vector
        def _(dve):
            def top_row(it, h, r):
                dve.wait_ge(scored, ROWS * (HB * it + h) + r + 1)
                wait(dve, exped, ROWS * (HB * it + h - 1) + r + 1)
                dve.tensor_reduce(top[:, r:r + 1], p_score[:, r % 2, 0:width_of(r)], AX_X, ALU.max,
                                  negate=True).then_inc(topped, 1)

            def rest(it, h, j):
                g, kb, c0 = block_of(j)
                slot = (BL * h + j) % PT
                dve.wait_ge(rounded, BL * (HB * it + h) + j + 1)
                dve.tensor_tensor(pt_lo[:, slot, c0:W], p_turn[:, (BL * h + j) % TB, c0:W], pt_hi[:, slot, c0:W].bitcast(F32),
                                  ALU.subtract).then_inc(split, 1)

            run({"engine": dve, "top": top_row, "rest": rest}, ORDER["vector"])


def project_out(nc, o_dram, total, ident, wo, v_bias, row, parked, res):
    QUADS = HEADS // 4
    BLK = W // P
    YB = 6
    with ExitStack() as ctx:
        sb, ps, sem = alloc(nc, ctx)
        raw = sb("wo_raw", [P, QUADS, D])
        w_hi = sb("wo_hi", [P, QUADS, D], F32R)
        w_lo = sb("wo_lo", [P, QUADS, D], F32R)
        o = sb("o", [P, 2, QUADS, 2, W])
        o_hi = sb("o_hi", [P, 2, QUADS, W], F32R)
        o_lo = sb("o_lo", [P, 2, QUADS, W], F32R)
        bias = sb("v_bias_sb", [P, QUADS])
        b_row = sb("bo_row", [P, D])
        inv = sb("inv", [P, QUADS, TT, BLK * 4])
        spread = sb("spread", [P, 2, BLK, P])
        p_y = ps("p_y", [P, YB, D])
        p_inv = ps("p_inv", [P, 2, W])
        w_loaded, b_loaded = sem("wo_loaded"), sem("bo_loaded")
        res_loaded = [sem(f"res_loaded{t}") for t in range(TT)]
        o_loaded = [sem(f"o_loaded{i}") for i in range(2)]
        w_rounded, w_split, res_biased = sem("wo_rounded"), sem("wo_split"), sem("res_biased2")
        o_rounded, o_split, y_done, y_added = sem("o_rounded"), sem("o_split"), sem("y_done"), sem("y_added")
        inverted, repeated, inv_turned, divided = sem("inverted"), sem("repeated"), sem("inv_turned"), sem("divided")
        summed = sem("summed")
        block = ctx.enter_context(nc.Block())

        @block.sync
        def _(sp):
            old = parked.rearrange("(n p) d -> p n d", p=P)
            for t in range(TT):
                if t >= 2:
                    sp.wait_ge(o_split, QUADS * (t - 1))
                for half in range(2):
                    sp.dma_start(o[:, t % 2, :, half], o_dram[:, half, :, t * W:(t + 1) * W].rearrange("q p t -> p q t"))\
                        .then_inc(o_loaded[t % 2], 16)
                if t == 0:
                    sp.dma_start(raw[:], wo).then_inc(w_loaded, 16)
                    sp.dma_start(bias[:], v_bias).then_inc(b_loaded, 16)
                    sp.dma_start(b_row[:], row.to_broadcast([P, D])).then_inc(b_loaded, 16)
                sp.dma_start(res[:, BLK * t:BLK * t + BLK], old[:, BLK * t:BLK * t + BLK]).then_inc(res_loaded[t], 16)

        @block.gpsimd
        def _(pool):
            def add_halves(t):
                pool.wait_ge(o_loaded[t % 2], 32 * (t // 2 + 1))
                for q in range(QUADS):
                    pool.tensor_tensor(o[:, t % 2, q, 0], o[:, t % 2, q, 0], o[:, t % 2, q, 1], ALU.add).then_inc(summed, 1)

            add_halves(0)
            pool.wait_ge(b_loaded, 32)
            for t in range(TT):
                if t + 1 < TT:
                    add_halves(t + 1)
                pool.wait_ge(res_loaded[t], 16)
                for i in range(BLK * t, BLK * t + BLK):
                    pool.tensor_tensor(res[:, i], res[:, i], b_row[:], ALU.add).then_inc(res_biased, 1)

        @block.scalar
        def _(act):
            def repeat(n):
                if n >= 2:
                    act.wait_ge(inv_turned, n - 1)
                act.activation(spread[:, n % 2].rearrange("p i (h e) -> p (i h) e", h=4),
                               inv[:, n % QUADS, n // QUADS].unsqueeze(2).to_broadcast([P, BLK * 4, E]),
                               ACT.Copy).then_inc(repeated, 1)

            act.wait_ge(inverted, 1)
            repeat(0)
            repeat(1)
            act.wait_ge(w_loaded, 16)
            act.activation(w_hi[:], raw[:], ACT.Copy).then_inc(w_rounded, 1)
            act.wait_ge(b_loaded, 32)
            for t in range(TT):
                if t >= 2:
                    act.wait_ge(y_done, BLK * (t - 1))
                for q in range(QUADS):
                    n = QUADS * t + q
                    if n + 2 < QUADS * TT:
                        repeat(n + 2)
                    act.wait_ge(divided, n + 1)
                    act.activation(o_hi[:, t % 2, q], o[:, t % 2, q, 0], ACT.Identity, bias=bias[:, q:q + 1]).then_inc(o_rounded, 1)

        @block.vector
        def _(dve):
            def add(t):
                for i in range(BLK * t, BLK * t + BLK):
                    dve.wait_ge(y_done, i + 1)
                    dve.wait_ge(res_biased, i + 1)
                    dve.tensor_tensor(res[:, i], res[:, i], p_y[:, i % YB], ALU.add).then_inc(y_added, 1)

            dve.reciprocal(inv[:].rearrange("p q t i -> p (q t i)"), total[:, :]).then_inc(inverted, 1)
            def divide(t, q):
                dve.wait_ge(inv_turned, QUADS * t + q + 1)
                dve.wait_ge(summed, QUADS * t + q + 1)
                dve.tensor_tensor(o[:, t % 2, q, 0], o[:, t % 2, q, 0], p_inv[:, q % 2], ALU.mult).then_inc(divided, 1)

            def keep_rest(t, q):
                dve.wait_ge(o_rounded, QUADS * t + q + 1)
                dve.scalar_tensor_tensor(o_lo[:, t % 2, q], o[:, t % 2, q, 0], bias[:, q:q + 1],
                                         o_hi[:, t % 2, q].bitcast(F32), ALU.add, ALU.subtract).then_inc(o_split, 1)

            for t in range(TT):
                divide(t, 0)
                for q in range(1, QUADS):
                    divide(t, q)
                    keep_rest(t, q - 1)
                if t == 0:
                    dve.wait_ge(w_rounded, 1)
                    dve.tensor_tensor(w_lo[:], raw[:], w_hi[:].bitcast(F32), ALU.subtract).then_inc(w_split, 1)
                keep_rest(t, QUADS - 1)
                if t:
                    add(t - 1)
            add(TT - 1)

        @block.tensor
        def _(pe):
            def turn_inverses(n):
                pe.wait_ge(repeated, n + 1)
                if n >= 2:
                    pe.wait_ge(divided, n - 1)
                for i in range(BLK):
                    mm = pe.transpose(p_inv[:, n % 2, i * P:(i + 1) * P], spread[:, n % 2, i], ident[:, :])
                mm.then_inc(inv_turned, 1)

            for q in range(QUADS):
                turn_inverses(q)
            pe.wait_ge(w_split, 1)
            for t in range(TT):
                pe.wait_ge(o_split, QUADS * (t + 1))
                for i in range(BLK * t, BLK * t + BLK):
                    if t + 1 < TT:
                        turn_inverses(QUADS * (t + 1) + i % BLK)
                    if i >= YB:
                        pe.wait_ge(y_added, i - YB + 1)
                    rows = slice(i % BLK * P, (i % BLK + 1) * P)
                    for q in range(QUADS):
                        pe.matmul(p_y[:, i % YB], o_hi[:, t % 2, q, rows], w_hi[:, q], start=(q == 0), stop=False)
                        pe.matmul(p_y[:, i % YB], o_hi[:, t % 2, q, rows], w_lo[:, q], start=False, stop=False)
                        mm = pe.matmul(p_y[:, i % YB], o_lo[:, t % 2, q, rows], w_hi[:, q], start=False,
                                       stop=(q == QUADS - 1))
                    mm.then_inc(y_done, 1)


def two_layers(nc, t, out):
    w2f = nc.dram_tensor("w2_rotated", [HID // P, P, D], F32, kind="Internal").ap()
    parked = nc.dram_tensor("res_parked", [T, D], F32, kind="Internal").ap()
    qk_dram = nc.dram_tensor("qk_parked", [HEADS // 2 * B, 2, P, S], F32, kind="Internal").ap()
    v_dram = nc.dram_tensor("v_parked", [HEADS // 4 * B, P, 8 * S // P * E], F32, kind="Internal").ap()
    o_dram = nc.dram_tensor("o_parked", [HEADS // 4, 2, P, T], F32, kind="Internal").ap()
    with ExitStack() as ctx:
        sb, _, _ = alloc(nc, ctx)
        ident = sb("ident", [P, P])
        x_hi = sb("x_hi", [P, KD, T], F32R)
        x_lo = sb("x_lo", [P, KD, T], F32R)
        with ExitStack() as layer0:
            res = alloc(nc, layer0)[0]("res0", [P, NT, D])
            with ExitStack() as front:
                n1 = alloc(nc, front)[0]("n1", [P, NT, D])
                phase(nc, prepare, t["x"], t["w2t"], t["signs"], t["eye"], w2f, ident, res, n1, x_hi, x_lo)
                phase(nc, state_space_branch, t["cols"], t["rank"], ident, res, n1)
            phase(nc, feed_forward, "ff0", t["wgu0"], w2f.rearrange("(g c) p d -> g c p d", c=NC), x_hi, x_lo, res, False,
                  parked, True)
            phase(nc, turn_and_split, res, ident, x_hi, x_lo)
        total = sb("total", [P, HEADS * NT])
        with ExitStack() as middle:
            sb1 = alloc(nc, middle)[0]
            stack = sb1("stack", [P, 2, 2, 2, S], F32R)
            v = sb1("v", [P, B, S // P, 4, 2, E], F32R)
            mask = sb1("mask", [P, 2, P], BF16)
            phase(nc, project_qkv, t["wqk"], t["wv"], t["qk_bias"], t["qk_scale"], t["masks"], x_hi, x_lo, qk_dram,
                  v_dram, stack, v, mask)
            phase(nc, attention, mask, stack, v, ident, qk_dram, v_dram, o_dram, total)
        with ExitStack() as layer1:
            res = alloc(nc, layer1)[0]("res1", [P, NT, D])
            phase(nc, project_out, o_dram, total, ident, t["wo"], t["v_bias"], t["bo"], parked, res)
            phase(nc, feed_forward, "ff1", t["wgu1"], t["wd1"], x_hi, x_lo, res, True, out, False)


def lay_out(inputs):
    import numpy as np

    a = {n: np.asarray(v) for n, v in inputs.items()}
    l0 = {n[8:]: v for n, v in a.items() if n.startswith("L0_attn_")}
    f32 = np.float32

    def by_chunk(w):
        return w.reshape(KD, P, -1).transpose(1, 0, 2).reshape(P, -1)

    def in_order(w):
        return w.reshape(KD, P, NG, NC, P).transpose(2, 3, 1, 0, 4)

    def by_four(w):
        return w.reshape(KD, P, NG, P, NC).transpose(2, 4, 1, 0, 3)

    hadamard = np.ones((1, 1), f32)
    while hadamard.shape[0] < P:
        hadamard = np.block([[hadamard, hadamard], [hadamard, -hadamard]])
    w_qkv, b_qkv = a["L1_attn_W_qkv"], a["L1_attn_b_qkv"]
    quads = HEADS // 4
    qk = w_qkv.T.reshape(KD, P, 3, quads, 2, 2 * E)[:, :, :2].transpose(3, 4, 1, 0, 2, 5)
    v = w_qkv.T.reshape(KD, P, 3, D)[:, :, 2].transpose(1, 0, 2)
    qk_scale = np.ones((P, 1), f32)
    qk_scale[:2 * E] = f32(1) / np.sqrt(f32(E))
    masks = np.zeros((P, 2, P), f32)
    masks[:, 0] = np.where(np.arange(P) > np.arange(P)[:, None], f32(-3e38), f32(0))
    masks[:, 1] = np.eye(P)
    arrays = {
        "x": a["L0_attn_x"].reshape(T, D),
        "w2t": a["L0_ffn_W2"].T,
        "signs": np.stack([hadamard, -hadamard], 1),
        "eye": np.eye(P, dtype=f32),
        "cols": np.concatenate([by_chunk(l0[n]) for n in ("ln_gamma", "ln_beta", "D_skip", "W_in", "W_down")], 1),
        "rank": np.concatenate([np.concatenate([l0[n][:, None] for n in ("b_in", "decay_logit", "b_down")] +
                                       [l0["W_out"], l0["W_up"]], 1),
                        np.concatenate([np.zeros(3, f32), l0["b_out"], l0["b_up"]])[None]]),
        "wgu0": np.stack([in_order(a["L0_ffn_W1"].T), in_order(a["L0_ffn_W3"].T)], 3),
        "wqk": qk.reshape(quads, 2, P, KD, P),
        "wv": v,
        "qk_bias": b_qkv.reshape(3, quads, 2, 2 * E)[:2].transpose(0, 3, 1, 2).reshape(P, 2 * quads),
        "qk_scale": qk_scale,
        "masks": masks,
        "wo": a["L1_attn_W_out"].T.reshape(quads, P, D).transpose(1, 0, 2),
        "v_bias": b_qkv[2 * D:].reshape(quads, P).T,
        "bo": a["L1_attn_b_out"][None],
        "wgu1": np.stack([by_four(a["L1_ffn_w_gate"]), by_four(a["L1_ffn_w_up"])], 3),
        "wd1": a["L1_ffn_w_down"].reshape(NG, P, NC, D).transpose(0, 2, 1, 3),
    }
    return {n: np.ascontiguousarray(v) for n, v in arrays.items()}


def kernel(**inputs):
    import concourse.bacc as bacc
    from concourse.bass_utils import run_bass_kernel_spmd

    nc = bacc.Bacc("TRN2", target_bir_lowering=False, num_devices=1)
    arrays = {f"in_{n}": v for n, v in lay_out(inputs).items()}
    aps = {n[3:]: nc.dram_tensor(n, v.shape, mybir.dt.from_np(v.dtype), kind="ExternalInput").ap() for n, v in arrays.items()}
    out = nc.dram_tensor("out_0", (T, D), F32, kind="ExternalOutput").ap()
    two_layers(nc, aps, out)
    got = run_bass_kernel_spmd(nc, [arrays], core_ids=[0])
    return got.results[0]["out_0"].reshape(B, S, D)
```
